# Optimizing a Trainium2 kernel written in Bass

```python
import numpy as np
import jax
import jax.numpy as jnp

def _softmax(x, axis=-1):
    return jax.nn.softmax(x, axis=axis)

def _gelu(x):
    return jax.nn.gelu(x, approximate=True)

def _silu(x):
    return jax.nn.silu(x)

def _sigmoid(x):
    return jax.nn.sigmoid(x)

def _layernorm(x, axis=-1, eps=1e-05):
    m = jnp.mean(x, axis=axis, keepdims=True)
    v = jnp.var(x, axis=axis, keepdims=True)
    return (x - m) / jnp.sqrt(v + eps)

def _scatter_add(tgt, idx, src, axis=0):
    return tgt.at[idx].add(src)

def _segment_sum(src, seg, n):
    return jax.ops.segment_sum(src, seg, n)
kernel_name = 'mk_macaron_d1_jaxref_r8_05fe4f'

def setup_inputs(seed: int=0):
    np.random.seed(seed)
    _w = jnp.asarray

    def _L0_attn_setup():
        import jax, jax.numpy as jnp
        import numpy as np
        D_MODEL = 128
        N_HEADS = 8
        N_KV_HEADS = 4
        HEAD_DIM = D_MODEL // N_HEADS
        N_REP = N_HEADS // N_KV_HEADS
        WINDOW = 128
        SINKS = 4
        ROPE_BASE = 10000.0
        SCALE = 1.0 / np.sqrt(HEAD_DIM)

        def _trigram_dirs():
            t = np.array([[s0, s1, s2] for s0 in (1.0, -1.0) for s1 in (1.0, -1.0) for s2 in (1.0, -1.0)], dtype=np.float32)
            t = t / np.linalg.norm(t, axis=1, keepdims=True)
            return jnp.asarray(t[:N_HEADS])

        def _rope_tables(T):
            inv_freq = 1.0 / ROPE_BASE ** (jnp.arange(0, HEAD_DIM, 2, dtype=jnp.float32) / HEAD_DIM)
            freqs = jnp.arange(T, dtype=jnp.float32)[:, None] * inv_freq[None, :]
            return (jnp.cos(freqs), jnp.sin(freqs))

        def _apply_rope(t, cos, sin):
            t1, t2 = jnp.split(t, 2, axis=-1)
            c = cos[None, None, :, :]
            s = sin[None, None, :, :]
            return jnp.concatenate([t1 * c - t2 * s, t2 * c + t1 * s], axis=-1)
        key = jax.random.key(seed)
        ks = jax.random.split(key, 6)
        B, T = (2, 256)
        std = 0.02
        x = jax.random.normal(ks[0], (B, T, D_MODEL), jnp.float32)
        Wq = jax.random.normal(ks[1], (D_MODEL, N_HEADS * HEAD_DIM), jnp.float32) * std
        Wk = jax.random.normal(ks[2], (D_MODEL, N_KV_HEADS * HEAD_DIM), jnp.float32) * std
        Wv = jax.random.normal(ks[3], (D_MODEL, N_KV_HEADS * HEAD_DIM), jnp.float32) * std
        Wo = jax.random.normal(ks[4], (D_MODEL, D_MODEL), jnp.float32) * std
        head_scales = jax.random.normal(ks[5], (N_HEADS,), jnp.float32) * 0.1
        head_dirs = _trigram_dirs()
        return {'x': x, 'Wq': Wq, 'Wk': Wk, 'Wv': Wv, 'Wo': Wo, 'head_scales': head_scales, 'head_dirs': head_dirs}
    _L0_attn_in = _L0_attn_setup()

    def _L0_ffn_setup():
        import jax, jax.numpy as jnp
        import numpy as np
        import math
        D_MODEL = 128
        N_EXPERTS = 16
        D_FF = 512
        CAP_FACTOR = 1.25
        MIN_CAPACITY = 4

        def _capacity(num_tokens, num_experts):
            cap = math.floor(CAP_FACTOR * num_tokens / num_experts)
            cap += cap % 2
            return max(cap, MIN_CAPACITY)

        def _top1_router(gate_logits, capacity):
            s, e = gate_logits.shape
            probs = jax.nn.softmax(gate_logits, axis=-1)
            top1 = jnp.argmax(gate_logits, axis=-1)
            mask = jax.nn.one_hot(top1, e, dtype=jnp.int32)
            ranks = jnp.cumsum(mask, axis=0) - 1
            mask = mask * (ranks < capacity).astype(jnp.int32)
            rank1 = jnp.sum(mask * ranks, axis=-1)
            ranks_oh = jax.nn.one_hot(rank1, capacity, dtype=probs.dtype)
            weight = mask.astype(probs.dtype) * probs
            combine_weights = weight[:, :, None] * ranks_oh[:, None, :]
            sec_mask = combine_weights > 0
            return (combine_weights, sec_mask)
        key = jax.random.key(seed)
        k1, k2, k3, k4 = jax.random.split(key, 4)
        x = jax.random.normal(k1, (4, 256, D_MODEL), dtype=jnp.float32)
        gate_w = jax.random.normal(k2, (N_EXPERTS, D_MODEL), dtype=jnp.float32) * math.sqrt(0.1 / D_MODEL)
        w1 = jax.random.normal(k3, (N_EXPERTS, D_MODEL, D_FF), dtype=jnp.float32) * (1.0 / math.sqrt(D_MODEL))
        w2 = jax.random.normal(k4, (N_EXPERTS, D_FF, D_MODEL), dtype=jnp.float32) * (1.0 / math.sqrt(D_FF))
        return {'x': x, 'gate_w': gate_w, 'w1': w1, 'w2': w2}
    _L0_ffn_in = _L0_ffn_setup()
    _d = {'L0_attn_x': _L0_attn_in['x'], 'L0_attn_Wq': _L0_attn_in['Wq'], 'L0_attn_Wk': _L0_attn_in['Wk'], 'L0_attn_Wv': _L0_attn_in['Wv'], 'L0_attn_Wo': _L0_attn_in['Wo'], 'L0_attn_head_scales': _L0_attn_in['head_scales'], 'L0_attn_head_dirs': _L0_attn_in['head_dirs'], 'L0_ffn_gate_w': _L0_ffn_in['gate_w'], 'L0_ffn_w1': _L0_ffn_in['w1'], 'L0_ffn_w2': _L0_ffn_in['w2']}
    _x0 = _d['L0_attn_x']
    _d['L0_attn_x'] = jax.random.normal(jax.random.fold_in(jax.random.key(seed), 1), (8, 512, 128), dtype=_x0.dtype)
    del _x0
    return _d

def reference(L0_attn_x, L0_attn_Wq, L0_attn_Wk, L0_attn_Wv, L0_attn_Wo, L0_attn_head_scales, L0_attn_head_dirs, L0_ffn_gate_w, L0_ffn_w1, L0_ffn_w2):

    def _L0_attn_ref(x, Wq, Wk, Wv, Wo, head_scales, head_dirs):
        import jax, jax.numpy as jnp
        import numpy as np
        D_MODEL = 128
        N_HEADS = 8
        N_KV_HEADS = 4
        HEAD_DIM = D_MODEL // N_HEADS
        N_REP = N_HEADS // N_KV_HEADS
        WINDOW = 128
        SINKS = 4
        ROPE_BASE = 10000.0
        SCALE = 1.0 / np.sqrt(HEAD_DIM)

        def _trigram_dirs():
            t = np.array([[s0, s1, s2] for s0 in (1.0, -1.0) for s1 in (1.0, -1.0) for s2 in (1.0, -1.0)], dtype=np.float32)
            t = t / np.linalg.norm(t, axis=1, keepdims=True)
            return jnp.asarray(t[:N_HEADS])

        def _rope_tables(T):
            inv_freq = 1.0 / ROPE_BASE ** (jnp.arange(0, HEAD_DIM, 2, dtype=jnp.float32) / HEAD_DIM)
            freqs = jnp.arange(T, dtype=jnp.float32)[:, None] * inv_freq[None, :]
            return (jnp.cos(freqs), jnp.sin(freqs))

        def _apply_rope(t, cos, sin):
            t1, t2 = jnp.split(t, 2, axis=-1)
            c = cos[None, None, :, :]
            s = sin[None, None, :, :]
            return jnp.concatenate([t1 * c - t2 * s, t2 * c + t1 * s], axis=-1)
        B, T, C = x.shape
        q = (x @ Wq).reshape(B, T, N_HEADS, HEAD_DIM).transpose(0, 2, 1, 3)
        k = (x @ Wk).reshape(B, T, N_KV_HEADS, HEAD_DIM).transpose(0, 2, 1, 3)
        v = (x @ Wv).reshape(B, T, N_KV_HEADS, HEAD_DIM).transpose(0, 2, 1, 3)
        cos, sin = _rope_tables(T)
        q = _apply_rope(q, cos, sin)
        k = _apply_rope(k, cos, sin)
        k = jnp.repeat(k, N_REP, axis=1)
        v = jnp.repeat(v, N_REP, axis=1)
        scores = jnp.einsum('bhtd,bhsd->bhts', q, k) * SCALE
        qp = jnp.einsum('bhtd,hd->bht', q[..., :3], head_dirs)
        kp = jnp.einsum('bhsd,hd->bhs', k[..., :3], head_dirs)
        scores = scores + head_scales[None, :, None, None] * (qp[..., :, None] * kp[..., None, :])
        i = jnp.arange(T)[:, None]
        j = jnp.arange(T)[None, :]
        allowed = (j <= i) & ((j < SINKS) | (j >= i - WINDOW + 1))
        scores = jnp.where(allowed[None, None, :, :], scores, -jnp.inf)
        attn = jax.nn.softmax(scores, axis=-1)
        out = jnp.einsum('bhts,bhsd->bhtd', attn, v)
        out = out.transpose(0, 2, 1, 3).reshape(B, T, C)
        return out @ Wo

    def _L0_ffn_ref(x, gate_w, w1, w2):
        import jax, jax.numpy as jnp
        import numpy as np
        import math
        D_MODEL = 128
        N_EXPERTS = 16
        D_FF = 512
        CAP_FACTOR = 1.25
        MIN_CAPACITY = 4

        def _capacity(num_tokens, num_experts):
            cap = math.floor(CAP_FACTOR * num_tokens / num_experts)
            cap += cap % 2
            return max(cap, MIN_CAPACITY)

        def _top1_router(gate_logits, capacity):
            s, e = gate_logits.shape
            probs = jax.nn.softmax(gate_logits, axis=-1)
            top1 = jnp.argmax(gate_logits, axis=-1)
            mask = jax.nn.one_hot(top1, e, dtype=jnp.int32)
            ranks = jnp.cumsum(mask, axis=0) - 1
            mask = mask * (ranks < capacity).astype(jnp.int32)
            rank1 = jnp.sum(mask * ranks, axis=-1)
            ranks_oh = jax.nn.one_hot(rank1, capacity, dtype=probs.dtype)
            weight = mask.astype(probs.dtype) * probs
            combine_weights = weight[:, :, None] * ranks_oh[:, None, :]
            sec_mask = combine_weights > 0
            return (combine_weights, sec_mask)
        tokens = x.reshape(-1, D_MODEL)
        s = tokens.shape[0]
        capacity = _capacity(s, N_EXPERTS)
        gate_logits = tokens.astype(jnp.float32) @ gate_w.T
        combine_weights, sec_mask = _top1_router(gate_logits, capacity)
        dispatch = jnp.einsum('sec,sd->ecd', sec_mask.astype(tokens.dtype), tokens)
        h = jax.nn.gelu(jnp.einsum('ecd,edf->ecf', dispatch, w1))
        expert_out = jnp.einsum('ecf,efd->ecd', h, w2)
        out = jnp.einsum('sec,ecd->sd', combine_weights.astype(tokens.dtype), expert_out)
        return out.reshape(x.shape)
    x = L0_attn_x
    x = x + 0.5 * _L0_ffn_ref(_layernorm(x, axis=-1), L0_ffn_gate_w, L0_ffn_w1, L0_ffn_w2)
    x = x + _L0_attn_ref(_layernorm(x, axis=-1), L0_attn_Wq, L0_attn_Wk, L0_attn_Wv, L0_attn_Wo, L0_attn_head_scales, L0_attn_head_dirs)
    x = x + 0.5 * _L0_ffn_ref(_layernorm(x, axis=-1), L0_ffn_gate_w, L0_ffn_w1, L0_ffn_w2)
    return x

_drawn_inputs = setup_inputs


def setup_inputs(seed=0):
    import zlib

    import numpy as np

    out = dict(_drawn_inputs(seed))
    spreads = {}
    factors = {'L0_attn_Wq': 8.0,
     'L0_attn_Wk': 8.0,
     'L0_attn_Wv': 8.0,
     'L0_attn_Wo': 8.0,
     'L0_attn_head_scales': 8.0,
     'L0_attn_head_dirs': 8.0}
    for name, (base, spread) in spreads.items():
        noise = np.random.default_rng([zlib.crc32(name.encode()), seed]).standard_normal(out[name].shape)
        drawn = base * np.exp(spread * noise) if base else spread * noise
        out[name] = jnp.asarray(drawn.astype(out[name].dtype))
    for name, factor in factors.items():
        out[name] = (out[name] * factor).astype(out[name].dtype)
    return out
```

```python
from contextlib import ExitStack

import numpy as np

import concourse.bass as bass
from concourse import mybir

F32 = mybir.dt.float32
BF16 = mybir.dt.bfloat16
I32 = mybir.dt.int32
ALU = mybir.AluOpType
ACT = mybir.ActivationFunctionType
X = mybir.AxisListType.X

P = 128
B, T, D = 8, 512, 128
TOKENS = B * T
TILES = TOKENS // P
TB = T // P
H, KV, HD = 8, 4, 16
G = H // KV
SINKS = 4
E, FF = 16, 512
CAP = 320
PAIRS = E // 2
HALF = P // 2
PC = 2 * CAP // P
FC = FF // P
ROW = D + 4
MEAN, RSTD, WEIGHT, TOKEN = D, D + 1, D + 2, D + 3
NOWHERE = 8000.0
EPS = 1e-5
SCALE = 0.25
MASKED = -1e30
Q_PARTS = (0, 0, 0, 1, 1, 2)
K_PARTS = (0, 1, 2, 0, 1, 0)
NP = len(Q_PARTS)
KR = NP * HD
MR = KV * 3
OC = H * (HD + 1)


def constants():
    p = np.arange(P)
    q = np.arange(P)
    f, cols = {}, {}

    def add(name, a):
        a = np.ascontiguousarray(a, np.float32).reshape(P, -1)
        f[name] = a
        cols[name] = a.shape[1]

    add("ident", np.eye(P))
    inv_freq = (np.float32(1.0) / np.float32(10000.0) ** (np.arange(0, HD, 2, dtype=np.float32) / np.float32(HD))).astype(np.float32)
    pos = (np.arange(TB)[None, :] * P + p[:, None]).astype(np.float32)
    ang = (pos[:, :, None] * inv_freq[None, None, :]).astype(np.float32)
    cos, sin = np.cos(ang), np.sin(ang)
    add("cos", np.concatenate([cos, cos], -1))
    add("sin", np.concatenate([-sin, sin], -1))
    add("descend", np.broadcast_to(E - np.arange(E), (P, E)))
    add("base", np.broadcast_to(np.arange(E) * CAP - 1, (P, E)))
    add("token", np.arange(TB)[None, :] * P + p[:, None])
    add("nhalf", np.full((P, TB), -0.5))
    row = np.arange(P)[:, None]
    add("own_head", ((row // SINKS) == (np.arange(OC) // (HD + 1))[None, :]))
    add("repeat", (np.arange(H * SINKS)[None, :] % SINKS) == row)
    h, hc = {}, {}

    def addh(name, a):
        h[name] = np.ascontiguousarray(a, np.float32).reshape(P, -1)
        hc[name] = h[name].shape[1]

    addh("identb", np.eye(P))
    prev = np.where(p[None, :] > q[:, None], 0.0, MASKED)
    own = np.where(p[None, :] <= q[:, None], 0.0, MASKED)
    addh("window", np.concatenate([prev, own], 1))
    addh("turned_window", np.concatenate([prev.T, own.T], 1))
    addh("sink1", np.where(np.arange(SINKS)[None, :] <= q[:, None], 0.0, MASKED))
    addh("upto", p[:, None] <= p[None, :])
    addh("ones", np.ones((P, P)))
    at, ath, o = {}, {}, 0
    for k, c in cols.items():
        at[k] = (o, o + c)
        o += c
    o = 0
    for k, c in hc.items():
        ath[k] = (o, o + c)
        o += c
    rows = np.zeros((MR, KV, T), np.float32)
    for r in range(MR):
        rows[r, r // 3] = 1.0
    fresh = np.zeros((P, PC, ROW), np.float32)
    fresh[:, :, TOKEN] = NOWHERE
    bf16 = mybir.dt.np(BF16)
    return (np.concatenate(list(f.values()), 1), at, np.concatenate(list(h.values()), 1).astype(bf16), ath,
            rows.astype(bf16), fresh)


class Count:

    def __init__(self, sem):
        self.sem, self.base, self.local, self.turn = sem, 0, 0, None

    def enter(self, turn, per):
        self.base, self.local, self.turn, self.per = self.value(), 0, turn, per

    def leave(self, turns):
        assert self.local == self.per, (self.sem, self.local, self.per)
        self.base, self.local, self.turn = self.base + turns * self.per, 0, None

    def value(self):
        at = self.base + self.local
        return at if self.turn is None else self.turn * self.per + at

    def up(self):
        self.local += 1
        return self.value()


class Bank:

    def __init__(self):
        self.last = None

    def take(self, eng, i, sem, reads, wait=lambda eng, s, value: eng.wait_ge(s, value)):
        if self.last is not None:
            s, value, at = self.last
            v = value(at if isinstance(at, int) == isinstance(i, int) else i - 1)
            if not isinstance(v, int) or v > 0:
                wait(eng, s, v)
        self.last = (sem, reads, i)

    def drain(self, eng, i):
        s, value, at = self.last
        eng.wait_ge(s, value(at if isinstance(at, int) else i - 1))


def macaron(nc, x, Wq, Wk, Wv, Wo, head_scales, head_dirs, gate_w, w1, w2, out):
    cf, at, ch, ath, kr_ones, fresh_rows = constants()
    cf_d = nc.inline_tensor(cf, "tables")
    ch_d = nc.inline_tensor(ch, "tables16")
    ones_d = nc.inline_tensor(kr_ones, "max_rows")
    fresh_d = nc.inline_tensor(fresh_rows, "fresh_rows")
    cf_d, ch_d, ones_d, fresh_d = (a.ap() if hasattr(a, "ap") and callable(a.ap) else a for a in (cf_d, ch_d, ones_d, fresh_d))

    slots_d = [nc.dram_tensor(f"slots{i}", (E * CAP, ROW), F32, kind="Internal").ap() for i in range(2)]
    x1_d = nc.dram_tensor("x1", (TOKENS, D), F32, kind="Internal").ap()
    x_rows = x.rearrange("b t d -> (b t) d")
    out_rows = out.rearrange("b t d -> (b t) d")
    x_b = x.rearrange("b (t p) d -> b p t d", p=P)
    x1_b = x1_d.rearrange("(b t p) d -> b p t d", p=P, t=TB)
    out_b = out.rearrange("b (t p) d -> b p t d", p=P)
    slots_p = [s.rearrange("(a p c) w -> a p c w", p=P, c=PC) for s in slots_d]
    w2_e = w2.rearrange("e (c p) d -> e p c d", p=P)

    ctx = ExitStack()
    with ctx:
        def sb(name, shape, dt=F32):
            return ctx.enter_context(nc.sbuf_tensor(name, shape, dt))

        def sem(name):
            return ctx.enter_context(nc.semaphore(name))

        cft = sb("cft", [P, cf.shape[1]])
        cht = sb("cht", [P, ch.shape[1]], BF16)
        tab = {k: cft[:, a:b] for k, (a, b) in at.items()}
        tab16 = {k: cht[:, a:b] for k, (a, b) in ath.items()}
        ident, identb = tab["ident"], tab16["identb"]
        cos4 = tab["cos"].rearrange("p (t d) -> p t d", t=TB)
        sin4 = tab["sin"].rearrange("p (t d) -> p t d", t=TB)
        fresh = sb("fresh", [P, PC, ROW])
        wqkv = sb("wqkv", [P, 2 * D])
        wo = sb("wo", [P, D])
        gw = sb("gw", [E, D])
        gwT = sb("gwT", [P, E])
        dirs = sb("dirs", [P, H, 3])
        hs4 = sb("hs4", [P, H])
        w1s = [sb(f"w1s{i}", [P, FF]) for i in range(2)]
        w2s = [sb(f"w2s{i}", [P, FC, D]) for i in range(2)]

        xall = sb("xall", [P, TILES, D])

        stats = sb("stats", [P, TB, 6])
        mv = sb("mv", [P, TB, 2])
        veps = sb("veps", [P, TB])
        rstd = sb("rstd", [P, TB])
        xn = sb("xn", [P, TB, D])
        xnT = sb("xnT", [P, TB, P])
        lmax = sb("lmax", [P, TB])
        ldiff = sb("ldiff", [P, TB, E])
        lexp = sb("lexp", [P, TB, E])
        lsum = sb("lsum", [P, TB])
        cand = sb("cand", [P, TB, E])
        first = sb("first", [P, TB])
        onehot = sb("onehot", [P, TB, E], BF16)
        place = sb("place", [P, TB, E])
        base = sb("base", [P, E])
        slot = sb("slot", [P, TB])
        limit = sb("limit", [P, TB])
        valid = sb("valid", [P, TB])
        tok_now = sb("tok_now", [P, TB])
        slot_i = [sb(f"slot_i{i}", [P, TB], I32) for i in range(2)]
        pay = [sb(f"pay{i}", [P, TB, ROW]) for i in range(2)]

        rows = sb("rows", [P, PAIRS, PC, ROW])
        en = sb("en", [P, PC, D])
        enT = sb("enT", [P, PC, P])
        hT = [sb(f"hT{i}", [P, FC, CAP]) for i in range(2)]
        yT = sb("yT", [P, PC, P])
        yrow = sb("yrow", [P, PC, D])
        ytok = sb("ytok", [P, PC], I32)

        astats = sb("astats", [P, TB, 6])
        amv = sb("amv", [P, TB, 2])
        aveps = sb("aveps", [P, TB])
        arstd = sb("arstd", [P, TB])
        an = sb("an", [P, TB, D])
        anT = sb("anT", [P, TB, P])
        qkv = sb("qkv", [P, TB, H + KV, HD])
        vall = sb("vall", [P, TILES, KV, HD])
        vaug = sb("vaug", [P, TB, KV, HD + 1])
        roped = sb("roped", [P, TB, H + KV, HD])
        rtmp = sb("rtmp", [P, TB, H + KV, HD])
        dprod = sb("dprod", [P, TB, H, 3])
        dsum = sb("dsum", [P, TB, H])
        dscaled = sb("dscaled", [P, TB, H])
        part1 = sb("part1", [P, TB, H + KV, HD], BF16)
        part2 = sb("part2", [P, TB, H + KV, HD], BF16)
        rest = sb("rest", [P, TB, H + KV, HD])
        qs = sb("qs", [P, TB, H, KR], BF16)
        ks = sb("ks", [P, TB, KV, KR], BF16)
        qT = sb("qT", [KR + MR, KV, G, TB, P], BF16)
        kT = sb("kT", [KR + MR, KV, TB, P], BF16)
        nmx = sb("nmx", [P, H])
        nsink = sb("nsink", [P, H])
        nm = sb("nm", [P, H])
        nrest = sb("nrest", [P, H])
        nm3 = sb("nm3", [P, G, KV, 3], BF16)
        psd = sb("psd", [P, H, SINKS])
        psk = [sb(f"psk{i}", [P, H * SINKS]) for i in range(2)]
        pskT = sb("pskT", [H * SINKS, P])
        vsink = sb("vsink", [H * SINKS, OC])
        probs = [sb(f"probs{i}", [P, KV, 2, G, P]) for i in range(2)]
        rden = sb("rden", [P, H])
        on = sb("on", [P, D])
        oT = sb("oT", [P, P])

        sc = [ctx.enter_context(nc.psum_tensor(f"sc{i}", [P, 2, 512], F32)) for i in range(2)]
        b4, b5, b6, b7 = (ctx.enter_context(nc.psum_tensor(f"b{i}", [P, 512], F32)) for i in (4, 5, 6, 7))
        hid = [sc[0][:, 0, 0:CAP], sc[0][:, 1, 0:CAP], sc[1][:, 0, 0:CAP], sc[1][:, 1, 0:CAP]]
        yps = [b6[:, 0:CAP], b7[:, 0:CAP]]
        b4h = b4[:, :].bitcast(BF16)
        b6h = b6[:, :].bitcast(BF16)

        tables_in = sem("tables_in")
        weights_in = sem("weights_in")
        fresh_in = sem("fresh_in")
        fresh_out = [sem("fresh_out0"), sem("fresh_out1")]
        x_in = [sem("x_in0"), sem("x_in1")]
        x_copied = sem("x_copied")
        x1_in = sem("x1_in")
        rows_in = sem("rows_in")
        w1_in = [sem("w1a_in"), sem("w1b_in")]
        w2_in = [sem("w2a_in"), sem("w2b_in")]
        out_written = sem("out_written")
        vec_chain = sem("vec_chain")
        pool_chain = sem("pool_chain")
        gw_turned = sem("gw_turned")
        gw_copied = sem("gw_copied")
        weights_scaled = sem("weights_scaled")
        r_var = sem("r_var")
        r_rstd = sem("r_rstd")
        r_xn = sem("r_xn")
        r_turned = sem("r_turned")
        r_xnT = sem("r_xnT")
        r_logits = sem("r_logits")
        r_diff = sem("r_diff")
        r_exp = sem("r_exp")
        r_onehot = sem("r_onehot")
        r_rank = sem("r_rank")
        r_based = sem("r_based")
        r_slots = sem("r_slots")
        r_payx = sem("r_payx")
        scattered = [sem("scattered0"), sem("scattered1")]
        e_xn = sem("e_xn")
        e_turned = sem("e_turned")
        e_xT = sem("e_xT")
        e_hid = sem("e_hid")
        e_gelu = sem("e_gelu")
        e_yps = [sem("e_yps0"), sem("e_yps1")]
        e_yT = [sem("e_yT0"), sem("e_yT1")]
        e_back = sem("e_back")
        e_rows = sem("e_rows")
        e_scattered = sem("e_scattered")
        a_var = sem("a_var")
        a_rstd = sem("a_rstd")
        a_xn = sem("a_xn")
        a_turned = sem("a_turned")
        a_xnT = sem("a_xnT")
        a_qkv = sem("a_qkv")
        a_qkv_copied = sem("a_qkv_copied")
        a_roped = sem("a_roped")
        a_stacked = sem("a_stacked")
        a_vs = sem("a_vs")
        a_vsink = sem("a_vsink")
        q_turned = sem("q_turned")
        q_copied = sem("q_copied")
        k_turned = sem("k_turned")
        k_copied = sem("k_copied")
        v_copied = sem("v_copied")
        s_ready = sem("s_ready")
        s_maxed = sem("s_maxed")
        sink_ready = sem("sink_ready")
        nm_split = sem("nm_split")
        nm_turned = sem("nm_turned")
        nm_copied = sem("nm_copied")
        ps_diff = sem("ps_diff")
        ps_exp = sem("ps_exp")
        ps_turned = sem("ps_turned")
        ps_copied = sem("ps_copied")
        st_ready = sem("st_ready")
        st_exp = sem("st_exp")
        pv_ready = sem("pv_ready")
        o_normed = sem("o_normed")
        o_turned = sem("o_turned")
        o_copied = sem("o_copied")
        wo_ready = sem("wo_ready")
        x_added = sem("x_added")

        N_WEIGHTS = 7
        ST = TB - 1

        def wait(eng, s, value):
            if not isinstance(value, int) or value > 0:
                eng.wait_ge(s, value)

        def wait_apart(eng, s, value):
            if isinstance(value, int):
                return wait(eng, s, value)
            value = eng.to_reg(value)
            eng.wait_ge(tables_in, 48)
            eng.wait_ge(s, value)

        def has(i, n):
            return not isinstance(i, int) or 0 <= i < n

        def sweep(eng, step, start, lo, hi, stop, counts=()):
            for i in range(start, lo):
                step(i)
            with eng.Fori(lo, hi) as i:
                for c, per in counts:
                    c.enter(i - lo, per)
                step(i)
            for c, per in counts:
                c.leave(hi - lo)
            for i in range(hi, stop):
                step(i)

        def sweep2(eng, step, start, lo, hi, stop, counts=()):
            for i in range(start, lo):
                step(i, i // 2, i % 2)
            with eng.Fori(lo // 2, hi // 2) as j:
                for c, per in counts:
                    c.enter(j - lo // 2, per)
                for u in range(2):
                    step(j * 2 + u, j, u)
            for c, per in counts:
                c.leave((hi - lo) // 2)
            for i in range(hi, stop):
                step(i, i // 2, i % 2)

        R_LO, R_HI = 2, B - 2
        E_LO, E_HI = 1, PAIRS - 1
        A_LO, A_HI = 2, B - 2

        def tiles(n, k):
            return xall[:, bass.ds(n, k), :]

        block = ctx.enter_context(nc.Block())

        @block.sync
        def _(sp):
            sp.dma_start(xall[:, 0:TB, :], x_b[0]).then_inc(x_in[0], 16)
            sp.dma_start(cft[:, :], cf_d).then_inc(tables_in, 16)
            sp.dma_start(gw[:, :], gate_w).then_inc(tables_in, 16)
            sp.dma_start(cht[:, :], ch_d).then_inc(tables_in, 16)
            sp.dma_start(fresh[:], fresh_d).then_inc(fresh_in, 16)
            sp.dma_start(xall[:, TB:2 * TB, :], x_b[1]).then_inc(x_in[1], 16)
            sp.wait_ge(fresh_in, 16)
            for a in range(PAIRS):
                sp.dma_start(slots_p[0][a], fresh[:]).then_inc(fresh_out[0], 16)
            for b in range(2, B):
                sp.wait_ge(x_in[b % 2], 16 * (b // 2))
                sp.dma_start(xall[:, TB * b:TB * (b + 1), :], x_b[b]).then_inc(x_in[b % 2], 16)
            for i in range(2):
                sp.dma_start(w1s[i][:, :], w1[i]).then_inc(w1_in[i], 16)
                sp.dma_start(w2s[i][:], w2_e[i]).then_inc(w2_in[i], 16)
            sp.dma_start(x1_d, x_rows).then_inc(x_copied, 16)
            sp.dma_start(wqkv[:, 0:D], Wq).then_inc(weights_in, 16)
            sp.dma_start(wqkv[:, D:D + KV * HD], Wk).then_inc(weights_in, 16)
            sp.dma_start(wqkv[:, D + KV * HD:2 * D], Wv).then_inc(weights_in, 16)
            sp.dma_start(wo[:, :], Wo).then_inc(weights_in, 16)
            sp.dma_start(dirs[:].rearrange("p h c -> p (h c)"),
                         head_dirs.rearrange("h c -> (h c)").unsqueeze(0).to_broadcast([P, H * 3])).then_inc(weights_in, 16)
            sp.dma_start(hs4[:, :], head_scales.unsqueeze(0).to_broadcast([P, H])).then_inc(weights_in, 16)
            sp.dma_start(kT[KR:KR + MR].rearrange("r k t p -> r k (t p)"), ones_d).then_inc(weights_in, 16)
            for a in range(PAIRS):
                sp.dma_start(slots_p[1][a], fresh[:]).then_inc(fresh_out[1], 16)

            def experts(phase):
                g0 = PAIRS * phase
                sp.wait_ge(scattered[0], 16 * TB * (4 + 8 * phase))
                sp.wait_ge(scattered[1], 16 * TB * 4)
                sp.wait_ge(fresh_out[phase], 16 * PAIRS)
                sp.dma_start(rows[:, 0], slots_p[phase][0]).then_inc(rows_in, 16)

                def step(p):
                    g = p + g0
                    first_pair, last_pair = isinstance(p, int) and p == 0, isinstance(p, int) and p == PAIRS - 1
                    if not last_pair:
                        sp.wait_ge(rows_in, (g + 1) * 16)
                        sp.dma_start(rows[:, bass.ds(p + 1, 1)], slots_p[phase][bass.ds(p + 1, 1)].rearrange("a p c w -> p a c w")).then_inc(rows_in, 16)
                    if not first_pair:
                        sp.wait_ge(e_yps[1], g)
                        sp.dma_start(w2s[1][:], w2_e[bass.ds(p * 2 + 1, 1)].rearrange("e p c d -> (e p) c d")).then_inc(w2_in[1], 16)
                    if last_pair and phase == 1:
                        return
                    nxt = 0 if last_pair else p * 2 + 2
                    sp.wait_ge(e_hid, (g * 2 + 1) * FC)
                    sp.dma_start(w1s[0][:, :], w1[bass.ds(nxt, 1)].rearrange("e p f -> (e p) f")).then_inc(w1_in[0], 16)
                    sp.wait_ge(e_hid, (g * 2 + 2) * FC)
                    sp.dma_start(w1s[1][:, :], w1[bass.ds(nxt + 1, 1)].rearrange("e p f -> (e p) f")).then_inc(w1_in[1], 16)
                    sp.wait_ge(e_yps[0], g + 1)
                    sp.dma_start(w2s[0][:], w2_e[bass.ds(nxt, 1)].rearrange("e p c d -> (e p) c d")).then_inc(w2_in[0], 16)

                sweep(sp, step, 0, E_LO, E_HI, PAIRS)
                if phase == 0:
                    sp.wait_ge(e_yps[1], PAIRS)
                    sp.dma_start(w2s[1][:], w2_e[1]).then_inc(w2_in[1], 16)

            experts(0)
            sp.wait_ge(x_copied, 16)
            sp.wait_ge(e_scattered, 16 * PC * PAIRS)
            for b in range(B):
                wait(sp, x1_in, 16 * b)
                sp.dma_start(xall[:, TB * b:TB * (b + 1), :], x1_b[b]).then_inc(x1_in, 16)
            for b in range(B):
                sp.wait_ge(x_added, TB * (b + 1))
                sp.dma_start(out_b[b], xall[:, TB * b:TB * (b + 1), :]).then_inc(out_written, 16)
            experts(1)
            sp.wait_ge(e_scattered, 2 * 16 * PC * PAIRS)

        @block.tensor
        def _(pe):
            mm, turn = nc.tensor.matmul, nc.tensor.transpose
            bank6, bank7 = Bank(), Bank()

            pe.wait_ge(tables_in, 48)
            bank6.take(pe, 0, gw_copied, lambda i: 1)
            turn(b6[:, 0:E], gw[:, :], ident[0:E, 0:E]).then_inc(gw_turned, 1)

            def r_turn(g, i, g_of):
                pe.wait_ge(r_xn, g + 1)
                bank6.take(pe, i, r_xnT, lambda i: g_of(i) + 1)
                for t in range(TB):
                    last = turn(b6[:, P * t:P * (t + 1)], xn[:, t, :], ident)
                last.then_inc(r_turned, 1)

            def r_logit(g, i, g_of):
                pe.wait_ge(r_xnT, g + 1)
                bank7.take(pe, i, r_diff, lambda i: g_of(i) + 1)
                for t in range(TB):
                    last = mm(b7[:, E * t:E * (t + 1)], xnT[:, t, :], gwT[:, :], start=(t == 0), stop=(t == TB - 1), skip_group_check=True)
                last.then_inc(r_logits, 1)

            def r_ranks(g, i, g_of):
                pe.wait_ge(r_onehot, g + 1)
                bank7.take(pe, i, r_based, lambda i: g_of(i) + 1)
                mm(b7[:, 0:TB * E], tab16["upto"], onehot[:].rearrange("p t e -> p (t e)"), start=True, stop=False, skip_group_check=True)
                for t in range(TB):
                    last = mm(b7[:, E * (t + 1):E * (TB + 1)].rearrange("p (t e) -> p t e", e=E), tab16["ones"],
                              onehot[:, t:t + 1, :].to_broadcast([P, TB - t, E]), start=False, stop=(t == TB - 1), skip_group_check=True)
                last.then_inc(r_rank, 1)

            def route_step(k, j, u):
                if has(k + 1, B):
                    r_turn(k + 1, k, lambda i: i + 1)
                if has(k, B):
                    r_ranks(k, k, lambda i: i)
                if has(k + 1, B):
                    r_logit(k + 1, k, lambda i: i + 1)

            sweep2(pe, route_step, -1, R_LO, R_HI, B)

            def experts(phase):
                g0 = PAIRS * phase

                def turn_in(p):
                    g = p + g0
                    pe.wait_ge(e_xn, g + 1)
                    wait(pe, e_rows, max(g - 2, g0) if isinstance(p, int) else g - 2)
                    for c in range(PC):
                        last = turn(b4[:, P * c:P * (c + 1)] if c < 4 else b5[:, 0:P], en[:, c, :], ident)
                    last.then_inc(e_turned, 1)

                def up(p, a):
                    g = p + g0
                    pe.wait_ge(w1_in[a], (g + 1) * 16)
                    if a == 0:
                        pe.wait_ge(e_xT, g + 1)
                    for f in range(FC):
                        wait(pe, e_gelu, (g * 2 + a - 1) * FC + f + 1)
                        mm(hid[f], w1s[a][:, P * f:P * (f + 1)], enT[:, :, HALF * a:HALF * (a + 1)],
                           start=True, stop=True).then_inc(e_hid, 1)

                def down(p, a):
                    g = p + g0
                    pe.wait_ge(w2_in[a], (g + 1) * 16)
                    wait(pe, e_yT[a], g)
                    for f in range(FC):
                        pe.wait_ge(e_gelu, (g * 2 + a) * FC + f + 1)
                        last = mm(yps[a], w2s[a][:, f, :], hT[a][:, f, :], start=(f == 0), stop=(f == FC - 1))
                    last.then_inc(e_yps[a], 1)

                def turn_back(p):
                    g = p + g0
                    for a in range(2):
                        pe.wait_ge(e_yT[a], g + 1)
                    if has(p + 2, PAIRS):
                        pe.wait_ge(e_xT, g + 3)
                    else:
                        pe.wait_ge(e_rows, g)
                    for c in range(PC):
                        last = turn(b4[:, P * c:P * (c + 1)] if c < 4 else b5[:, 0:P], yT[:, c, :], ident)
                    last.then_inc(e_back, 1)

                def step(p):
                    if has(p, PAIRS):
                        up(p, 0)
                    if has(p - 1, PAIRS):
                        down(p - 1, 1)
                    if has(p, PAIRS):
                        up(p, 1)
                    if has(p + 1, PAIRS):
                        turn_in(p + 1)
                    if has(p, PAIRS):
                        down(p, 0)
                    if has(p - 1, PAIRS):
                        turn_back(p - 1)

                sweep(pe, step, -1, E_LO, E_HI, PAIRS + 1)

            bank6.drain(pe, 0)
            bank7.drain(pe, 0)
            experts(0)
            pe.wait_ge(e_gelu, 2 * PAIRS * FC)
            pe.wait_ge(e_rows, PAIRS)
            for a in range(2):
                pe.wait_ge(e_yT[a], PAIRS)
            pe.wait_ge(weights_in, 16 * N_WEIGHTS)
            pe.wait_ge(weights_scaled, 1)

            def a_turn(bb, b):
                pe.wait_ge(a_xn, bb + 1)
                bank6.take(pe, b, a_xnT, lambda b: b + 3)
                for t in range(TB):
                    last = turn(b6[:, P * t:P * (t + 1)], an[:, t, :], ident)
                last.then_inc(a_turned, 1)

            def a_project(bb, b, half):
                pe.wait_ge(a_xnT, bb + 1)
                bank6.take(pe, b, a_qkv_copied, lambda b: (b + 2) * 2 + half + 1)
                for u in range(2):
                    last = mm(b6[:, 2 * D * u:2 * D * (u + 1)], anT[:, 2 * half + u, :], wqkv[:, :],
                              start=(u == 0), stop=(u == 1), skip_group_check=True)
                last.then_inc(a_qkv, 1)

            def turn_q(n, t, bb):
                pe.wait_ge(a_stacked, bb + 1)
                wait(pe, k_copied, n)
                for h in range(H):
                    last = turn(b4h[0:KR, P * h:P * (h + 1)], qs[:, t, h, :], identb)
                last.then_inc(q_turned, 1)

            def turn_k(n, t):
                pe.wait_ge(q_copied, n + 1)
                for j in range(KV):
                    last = turn(b4h[0:KR, P * j:P * (j + 1)], ks[:, t, j, :], identb)
                last.then_inc(k_turned, 1)

            def scores(n, t):
                pe.wait_ge(k_copied, n + 1)
                lo = 0 if t else P
                for h in range(2):
                    wait(pe, st_exp, n * 2 + h - 3)
                    for jj in range(2):
                        j = 2 * h + jj
                        bank = sc[h][:, jj, :].rearrange("p (g k) -> p g k", g=G)
                        mm(bank[:, :, lo:2 * P], identb, tab16["window"][:, lo:2 * P].unsqueeze(1).to_broadcast([P, G, 2 * P - lo]),
                           start=True, stop=False, skip_group_check=True)
                        for g in range(G):
                            last = mm(bank[:, g, lo:2 * P], qT[0:KR, j, g, t, :],
                                      kT[0:KR, j, t - 1:t + 1, :] if t else kT[0:KR, j, t, :],
                                      start=False, stop=(g == G - 1), skip_group_check=True)
                    last.then_inc(s_ready, 1)

            def sink_scores(t, b):
                bank7.take(pe, b, ps_diff, lambda b: b * ST + t)
                cols = b7[:, 0:H * SINKS].rearrange("p (h s) -> p h s", s=SINKS)
                if t == 1:
                    mm(cols, identb, tab16["sink1"].unsqueeze(1).to_broadcast([P, H, SINKS]), start=True, stop=False, skip_group_check=True)
                for h in range(H):
                    last = mm(cols[:, h, :], qT[0:KR, h // G, h % G, t, :], kT[0:KR, h // G, 0, 0:SINKS],
                              start=(t > 1 and h == 0), stop=(h == H - 1), skip_group_check=True)
                last.then_inc(sink_ready, 1)

            def turned_scores(n, t, h, more):
                pe.wait_ge(nm_copied, n + 1)
                if more:
                    pe.wait_ge(s_maxed, (n + 1) * 2 + h + 1)
                for jj in range(2):
                    j = 2 * h + jj
                    bank = sc[h][:, jj, :].rearrange("p (b g q) -> p b g q", b=2, g=G)
                    lo = 0 if t else 1
                    mm(bank[:, lo:], identb, tab16["turned_window"].rearrange("p (b q) -> p b q", b=2)[:, lo:].unsqueeze(2).to_broadcast([P, 2 - lo, G, P]),
                       start=True, stop=False, skip_group_check=True)
                    for kb in range(lo, 2):
                        last = mm(bank[:, kb], kT[:, j, t - 1 + kb, :], qT[:, j, :, t, :], start=False, stop=(kb == 1), skip_group_check=True)
                last.then_inc(st_ready, 1)

            def turn_max(n, b, d):
                pe.wait_ge(nm_split, n + 1)
                bank6.take(pe, b, nm_copied, lambda b: b * TB + d + 1)
                for g in range(G):
                    last = turn(b6h[KR:KR + MR, P * g:P * (g + 1)], nm3[:, g].rearrange("p k c -> p (k c)"), identb)
                last.then_inc(nm_turned, 1)

            def turn_sinks(t, b):
                pe.wait_ge(ps_exp, b * ST + t)
                bank6.take(pe, b, ps_copied, lambda b: b * ST + t)
                turn(b6[0:H * SINKS, 0:P], psk[t % 2][:, :], ident).then_inc(ps_turned, 1)

            def sink_values(b):
                bank7.take(pe, b, a_vsink, lambda b: b + 1, wait_apart)
                pe.wait_ge(v_copied, b * TB + 1)
                mm(b7[0:H * SINKS, 0:OC], tab["repeat"][0:SINKS, :],
                   vaug[0:SINKS, 0, :, :].unsqueeze(2).to_broadcast([SINKS, KV, G, HD + 1]), start=True, stop=True).then_inc(a_vs, 1)

            def values(n, t, h, bb):
                if h == 0:
                    pe.wait_ge(v_copied, n + 1)
                    wait(pe, o_normed, n)
                    if t:
                        pe.wait_ge(ps_copied, bb * ST + t)
                        pe.wait_ge(a_vsink, bb + 1)
                        mm(b5[:, 0:OC], pskT[:, :], vsink[:, :], start=True, stop=False, skip_group_check=True)
                pe.wait_ge(st_exp, n * 2 + h + 1)
                for j in (2 * h, 2 * h + 1):
                    for g in range(G):
                        hh = G * j + g
                        for kb in range(0 if t else 1, 2):
                            last = mm(b5[:, (HD + 1) * hh:(HD + 1) * (hh + 1)], probs[t % 2][:, j, kb, g, :], vaug[:, t - 1 + kb, j, :],
                                      start=(t == 0 and hh == 0), stop=(hh == H - 1 and kb == 1), skip_group_check=True)
                if h == 1:
                    last.then_inc(pv_ready, 1)

            def turn_out(n, b, d):
                pe.wait_ge(o_normed, n + 1)
                bank6.take(pe, b, o_copied, lambda b: b * TB + d + 1)
                turn(b6[:, 0:P], on[:, :], ident).then_inc(o_turned, 1)

            def project(n, b, d):
                pe.wait_ge(o_copied, n + 1)
                bank7.take(pe, b, x_added, lambda b: b * TB + d + 1)
                mm(b7[:, 0:D], oT[:, :], wo[:, :], start=True, stop=True).then_inc(wo_ready, 1)

            def step(b):
                for t in range(TB):
                    k = b * TB + t
                    c, d, e, f = k + 1, k + 2, k - 1, k - 2
                    tc, td, te = (t + 1) % TB, (t + 2) % TB, (t - 1) % TB
                    if t == 2 and has(b + 2, B):
                        a_turn(b + 2, b)
                    if has(c, TILES):
                        scores(c, tc)
                        if tc:
                            sink_scores(tc, b)
                    if has(f, TILES):
                        turn_out(f, b, t - 2)
                    if has(d, TILES):
                        turn_q(d, td, b + (t + 2) // TB)
                    if t == 2 and has(b + 2, B):
                        a_project(b + 2, b, 0)
                    if t == 1 and has(b, B):
                        sink_values(b)
                    if has(k, TILES):
                        turned_scores(k, t, 0, has(c, TILES))
                    if has(e, TILES):
                        values(e, te, 0, b + (t - 1) // TB)
                    if has(k, TILES):
                        turned_scores(k, t, 1, has(c, TILES))
                    if has(d, TILES):
                        turn_k(d, td)
                    if t == 2 and has(b + 2, B):
                        a_project(b + 2, b, 1)
                    if has(e, TILES):
                        values(e, te, 1, b + (t - 1) // TB)
                    if has(c, TILES):
                        turn_max(c, b, t + 1)
                    if has(k, TILES) and t:
                        turn_sinks(t, b)
                    if t == 2 and has(b - 1, B):
                        r_turn(b - 1 + B, b, lambda i: i - 1 + B)
                    if has(f, TILES):
                        project(f, b, t - 2)
                    if t == 2 and has(b - 1, B):
                        r_logit(b - 1 + B, b, lambda i: i - 1 + B)
                    if t == 3 and has(b - 1, B):
                        r_ranks(b - 1 + B, b, lambda i: i - 1 + B)

            sweep(pe, step, -2, A_LO, A_HI, B + 1)
            pe.wait_ge(st_exp, 2 * TILES)
            pe.wait_ge(o_normed, TILES)
            pe.wait_ge(k_copied, TILES)
            bank6.drain(pe, 0)
            bank7.drain(pe, 0)
            experts(1)

        @block.scalar
        def _(act):
            act.wait_ge(gw_turned, 1)
            nc.scalar.copy(gwT[:, :], b6[:, 0:E]).then_inc(gw_copied, 1)

            def r_copy(g):
                act.wait_ge(r_turned, g + 1)
                wait(act, r_logits, g)
                nc.scalar.copy(xnT[:].rearrange("p t c -> p (t c)"), b6[:, :]).then_inc(r_xnT, 1)

            def r_exps(g):
                act.wait_ge(r_diff, g + 1)
                nc.scalar.activation(lexp[:].rearrange("p t e -> p (t e)"), ldiff[:].rearrange("p t e -> p (t e)"), ACT.Exp).then_inc(r_exp, 1)

            def route_step(k, j, u):
                if has(k + 1, B):
                    r_copy(k + 1)
                if has(k, B):
                    r_exps(k)
                if has(k + 1, B):
                    v, before = (u + 1) % 2, j + u
                    act.wait_ge(x_in[v], before * 16 + 16)
                    wait(act, scattered[v], before * (16 * TB))
                    nc.scalar.copy(pay[v][:, :, 0:D], tiles((k + 1) * TB, TB)).then_inc(r_payx, 1)

            sweep2(act, route_step, -1, R_LO, R_HI, B)

            def experts(phase):
                g0 = PAIRS * phase

                def gelus(p, a):
                    g = p + g0
                    wait(act, e_yps[a], g)
                    for f in range(FC):
                        act.wait_ge(e_hid, (g * 2 + a) * FC + f + 1)
                        nc.scalar.activation(hT[a][:, f, :], hid[f], ACT.Gelu_apprx_tanh).then_inc(e_gelu, 1)

                def y_copy(p, a):
                    g = p + g0
                    act.wait_ge(e_yps[a], g + 1)
                    wait(act, e_back, g)
                    nc.scalar.copy(yT[:, :, HALF * a:HALF * (a + 1)], yps[a].rearrange("p (c q) -> p c q", c=PC)).then_inc(e_yT[a], 1)

                def step(p):
                    if has(p, PAIRS):
                        gelus(p, 0)
                    if has(p - 1, PAIRS):
                        y_copy(p - 1, 1)
                    if has(p, PAIRS):
                        gelus(p, 1)
                        y_copy(p, 0)

                sweep(act, step, 0, E_LO, E_HI, PAIRS + 1)

            experts(0)

            def qkv_copy(bb, half):
                act.wait_ge(a_qkv, bb * 2 + half + 1)
                wait(act, a_roped, bb)
                ps = b6[:, :].rearrange("p (u h d) -> p u h d", u=2, d=HD)
                nc.scalar.copy(qkv[:, 2 * half:2 * half + 2], ps[:, :, 0:H + KV])
                nc.scalar.copy(vall[:, bass.ds(bb * TB + 2 * half, 2)].rearrange("p u k d -> p u (k d)"),
                               b6[:, :].rearrange("p (u c) -> p u c", u=2)[:, :, D + KV * HD:]).then_inc(a_qkv_copied, 1)

            def step(b):
                for t in range(TB):
                    k = b * TB + t
                    c, d, f = k + 1, k + 2, k - 2
                    tc, td = (t + 1) % TB, (t + 2) % TB
                    if t == 2 and has(b + 2, B):
                        act.wait_ge(a_turned, b + 3)
                        wait(act, a_qkv, (b + 2) * 2)
                        nc.scalar.copy(anT[:].rearrange("p t c -> p (t c)"), b6[:, :]).then_inc(a_xnT, 1)
                    if has(f, TILES):
                        act.wait_ge(o_turned, f + 1)
                        wait(act, wo_ready, f)
                        nc.scalar.copy(oT[:, :], b6[:, 0:P]).then_inc(o_copied, 1)
                    if has(d, TILES):
                        act.wait_ge(q_turned, d + 1)
                        nc.scalar.copy(qT[0:KR, :, :, td, :].rearrange("r k g q -> r (k g) q"),
                                       b4h[0:KR, :].rearrange("r (h q) -> r h q", h=H)).then_inc(q_copied, 1)
                    if t == 2 and has(b + 2, B):
                        qkv_copy(b + 2, 0)
                    if has(k, TILES):
                        for h in range(2):
                            act.wait_ge(st_ready, k * 2 + h + 1)
                            wait(act, pv_ready, k - 1)
                            if t:
                                nc.scalar.activation(probs[t % 2][:, 2 * h:2 * h + 2].rearrange("p j b g q -> p j (b g q)"),
                                                     sc[h][:], ACT.Exp).then_inc(st_exp, 1)
                            else:
                                nc.scalar.activation(probs[0][:, 2 * h:2 * h + 2, 1].rearrange("p j g q -> p j (g q)"),
                                                     sc[h][:, :, G * P:2 * G * P], ACT.Exp).then_inc(st_exp, 1)
                    if has(d, TILES):
                        act.wait_ge(k_turned, d + 1)
                        nc.scalar.copy(kT[0:KR, :, td, :], b4h[0:KR, 0:KV * P].rearrange("r (k q) -> r k q", k=KV)).then_inc(k_copied, 1)
                    if t == 2 and has(b + 2, B):
                        qkv_copy(b + 2, 1)
                    if has(c, TILES):
                        act.wait_ge(nm_turned, c + 1)
                        nc.scalar.copy(qT[KR:KR + MR, :, :, tc, :].rearrange("r k g q -> r g k q"),
                                       b6h[KR:KR + MR, 0:G * P].rearrange("r (g q) -> r g q", g=G).unsqueeze(2).to_broadcast([MR, G, KV, P])).then_inc(nm_copied, 1)
                        if tc:
                            act.wait_ge(ps_diff, b * ST + tc)
                            wait(act, ps_turned, b * ST + tc - 2)
                            nc.scalar.activation(psk[tc % 2][:, :], psd[:].rearrange("p h s -> p (h s)"), ACT.Exp).then_inc(ps_exp, 1)
                    if has(k, TILES) and t:
                        act.wait_ge(ps_turned, b * ST + t)
                        wait(act, pv_ready, k)
                        nc.scalar.copy(pskT[:, :], b6[0:H * SINKS, 0:P]).then_inc(ps_copied, 1)
                    if has(b - 1, B):
                        if t == 2:
                            r_copy(b - 1 + B)
                            act.wait_ge(x_added, b * TB)
                            wait(act, scattered[0], (b - 1) * (16 * TB) + 16 * TB * 4)
                            nc.scalar.copy(pay[0][:, :, 0:D], tiles((b - 1) * TB, TB)).then_inc(r_payx, 1)
                        if t == 3:
                            r_exps(b - 1 + B)

            sweep(act, step, -2, A_LO, A_HI, B + 1)
            experts(1)

        @block.vector
        def _(dve):
            v = nc.vector
            chain = Count(vec_chain)

            def link(ins, wait=wait):
                ins.then_inc(vec_chain, 1)
                wait(dve, vec_chain, chain.up())

            dve.wait_ge(tables_in, 48)

            def fresh_ranks():
                v.tensor_copy(base[:, :], tab["base"])
                link(v.tensor_copy(tok_now[:, :], tab["token"]))

            def means(n0, st, m, ve, done):
                for t in range(TB):
                    ins = v.bn_stats(st[:, t, :], tiles(n0 + t, 1).rearrange("p a d -> p (a d)"))
                link(ins, wait_apart)
                for t in range(TB):
                    ins = v.bn_aggr(m[:, t, :], st[:, t, :])
                link(ins)
                v.tensor_scalar(ve[:, :], m[:, :, 1], EPS, None, ALU.add).then_inc(done, 1)

            def normalise(n0, dst, m, r, done):
                for t in range(TB):
                    ins = v.tensor_scalar(dst[:, t, :], tiles(n0 + t, 1).rearrange("p a d -> p (a d)"),
                                          m[:, t, 0:1], r[:, t:t + 1], ALU.subtract, ALU.mult)
                ins.then_inc(done, 1)

            def r_norm(g, n0, s):
                dve.wait_ge(r_rstd, g + 1)
                wait(dve, r_turned, g)
                normalise(n0, xn, mv, rstd, r_xn)
                v.tensor_copy(pay[s][:, :, MEAN], mv[:, :, 0])
                v.tensor_copy(pay[s][:, :, RSTD], rstd[:, :])

            def r_route(g, s):
                logits = b7[:, 0:TB * E].rearrange("p (t e) -> p t e", e=E)
                dve.wait_ge(r_logits, g + 1)
                link(v.tensor_reduce(lmax[:, :], logits, X, ALU.max))
                v.tensor_tensor(ldiff[:], logits, lmax[:, :].unsqueeze(2).to_broadcast([P, TB, E]), ALU.subtract).then_inc(r_diff, 1)
                dve.wait_ge(r_diff, g + 1)
                link(v.scalar_tensor_tensor(cand[:], ldiff[:], 0.0, tab["descend"].unsqueeze(1).to_broadcast([P, TB, E]), ALU.is_equal, ALU.mult))
                link(v.tensor_reduce(first[:, :], cand[:], X, ALU.max))
                v.tensor_tensor(onehot[:], cand[:], first[:, :].unsqueeze(2).to_broadcast([P, TB, E]), ALU.is_equal).then_inc(r_onehot, 1)
                dve.wait_ge(r_exp, g + 1)
                link(v.tensor_reduce(lsum[:, :], lexp[:], X, ALU.add))
                link(v.tensor_scalar(lsum[:, :], lsum[:, :], 2.0, None, ALU.mult))
                v.reciprocal(pay[s][:, :, WEIGHT], lsum[:, :])

            def r_place(g, s):
                dve.wait_ge(r_rank, g + 1)
                v.tensor_copy(pay[s][:, :, TOKEN], tok_now[:, :])
                link(v.tensor_tensor(place[:], b7[:, 0:TB * E].rearrange("p (t e) -> p t e", e=E),
                                     base[:, :].unsqueeze(1).to_broadcast([P, TB, E]), ALU.add))
                v.tensor_tensor(base[:, :], b7[:, TB * E:(TB + 1) * E], base[:, :], ALU.add).then_inc(r_based, 1)
                v.tensor_scalar(tok_now[:, :], tok_now[:, :], float(T), None, ALU.add)
                link(v.tensor_tensor(place[:], place[:], onehot[:], ALU.mult))
                v.tensor_scalar(limit[:, :], first[:, :], -float(CAP), float((E + 1) * CAP), ALU.mult, ALU.add)
                link(v.tensor_reduce(slot[:, :], place[:], X, ALU.add))
                link(v.tensor_tensor(valid[:, :], slot[:, :], limit[:, :], ALU.is_lt))
                link(v.scalar_tensor_tensor(slot[:, :], slot[:, :], NOWHERE, valid[:, :], ALU.subtract, ALU.mult))
                v.tensor_scalar(slot_i[s][:, :], slot[:, :], NOWHERE, None, ALU.add).then_inc(r_slots, 1)

            def route_step(k, j, u):
                if has(k + 1, B):
                    vv, before = (u + 1) % 2, j + u
                    wait(dve, scattered[vv], before * (16 * TB))
                    r_norm(k + 1, (k + 1) * TB, vv)
                if has(k + 2, B):
                    dve.wait_ge(x_in[u], j * 16 + 32)
                    means((k + 2) * TB, stats, mv, veps, r_var)
                if has(k, B):
                    r_route(k, u)
                    r_place(k, u)

            fresh_ranks()
            sweep2(dve, route_step, -2, R_LO, R_HI, B, [(chain, 2 * ROUTE_LINKS)])

            def experts(phase):
                g0 = PAIRS * phase

                def norm(p):
                    g = p + g0
                    dve.wait_ge(rows_in, (g + 1) * 16)
                    wait(dve, e_turned, g)
                    for c in range(PC):
                        r = rows[:, bass.ds(p, 1), c, :].rearrange("p a w -> p (a w)")
                        ins = v.tensor_scalar(en[:, c, :], r[:, 0:D], r[:, MEAN:MEAN + 1], r[:, RSTD:RSTD + 1], ALU.subtract, ALU.mult)
                    ins.then_inc(e_xn, 1)

                def copy_in(p):
                    g = p + g0
                    dve.wait_ge(e_turned, g + 1)
                    wait(dve, e_hid, g * (2 * FC))
                    v.tensor_copy(enT[:, 0:4, :].rearrange("p c q -> p (c q)"), b4[:, :])
                    v.tensor_copy(enT[:, 4, :], b5[:, 0:P]).then_inc(e_xT, 1)

                def add_back(p):
                    g = p + g0
                    wait(dve, e_scattered, g * (16 * PC))
                    r = rows[:, bass.ds(p, 1)].rearrange("p a c w -> p (a c) w")
                    v.tensor_copy(ytok[:, :], r[:, :, TOKEN])
                    dve.wait_ge(e_back, g + 1)
                    for c in range(PC):
                        ins = v.scalar_tensor_tensor(yrow[:, c, :], b4[:, P * c:P * (c + 1)] if c < 4 else b5[:, 0:P],
                                                     r[:, c, WEIGHT:WEIGHT + 1], r[:, c, 0:D], ALU.mult, ALU.add)
                    ins.then_inc(e_rows, 1)

                def step(p):
                    if has(p + 1, PAIRS):
                        norm(p + 1)
                        copy_in(p + 1)
                    if has(p - 1, PAIRS):
                        add_back(p - 1)

                sweep(dve, step, -1, E_LO, E_HI, PAIRS + 1)

            experts(0)
            dve.wait_ge(weights_in, 16 * N_WEIGHTS)
            v.tensor_scalar(wqkv[:, 0:D], wqkv[:, 0:D], SCALE, None, ALU.mult)
            v.tensor_scalar(hs4[:, :], hs4[:, :], 1.0 / SCALE, None, ALU.mult).then_inc(weights_scaled, 1)
            dve.wait_ge(weights_scaled, 1)
            fresh_ranks()

            def maxima(n, t, b):
                for h in range(2):
                    dve.wait_ge(s_ready, n * 2 + h + 1)
                    s4 = sc[h][:].rearrange("p j (g k) -> p j g k", g=G)
                    v.tensor_reduce(nmx[:, 4 * h:4 * h + 4].rearrange("p (j g) -> p j g", g=G), s4 if t else s4[:, :, :, P:2 * P],
                                    X, ALU.max, negate=True).then_inc(s_maxed, 1)
                sinks = b7[:, 0:H * SINKS].rearrange("p (h s) -> p h s", s=SINKS)
                if t:
                    dve.wait_ge(sink_ready, b * ST + t)
                    link(v.tensor_reduce(nsink[:, :], sinks, X, ALU.max, negate=True))
                    link(v.tensor_tensor(nm[:, :], nmx[:, :], nsink[:, :], ALU.min))
                    m = nm
                else:
                    dve.wait_ge(s_maxed, n * 2 + 2)
                    m = nmx
                wait(dve, nm_turned, n)
                m3 = nm3[:].rearrange("p g k c -> p k g c")
                mg = m[:, :].rearrange("p (k g) -> p k g", g=G)
                rg = nrest[:, :].rearrange("p (k g) -> p k g", g=G)
                link(v.tensor_copy(m3[:, :, :, 0], mg))
                link(v.tensor_tensor(rg, mg, m3[:, :, :, 0], ALU.subtract))
                link(v.tensor_copy(m3[:, :, :, 1], rg))
                v.tensor_tensor(m3[:, :, :, 2], rg, m3[:, :, :, 1], ALU.subtract).then_inc(nm_split, 1)
                if t:
                    wait(dve, ps_exp, b * ST + t - 1)
                    v.tensor_tensor(psd[:], sinks, nm[:, :].unsqueeze(2).to_broadcast([P, H, SINKS]), ALU.add).then_inc(ps_diff, 1)

            def bend(bb):
                dve.wait_ge(a_roped, bb + 1)
                q3 = roped[:, :, 0:H, 0:3]
                d4 = dirs[:].unsqueeze(1).to_broadcast([P, TB, H, 3])
                link(v.tensor_tensor(dprod[:], q3, d4, ALU.mult))
                link(v.tensor_reduce(dsum[:], dprod[:], X, ALU.add))
                link(v.tensor_tensor(dscaled[:], dsum[:], hs4[:, :].unsqueeze(1).to_broadcast([P, TB, H]), ALU.mult))
                link(v.tensor_tensor(dprod[:], dscaled[:].unsqueeze(3).to_broadcast([P, TB, H, 3]), d4, ALU.mult))
                link(v.tensor_tensor(q3, q3, dprod[:], ALU.add))
                link(v.tensor_copy(part1[:], roped[:]))
                link(v.tensor_tensor(rest[:], roped[:], part1[:], ALU.subtract))

            def stack(bb, n):
                link(v.tensor_copy(part2[:], rest[:]))
                wait(dve, k_turned, n)
                q5 = qs[:].rearrange("p t h (s d) -> p t h s d", s=NP)
                k5 = ks[:].rearrange("p t h (s d) -> p t h s d", s=NP)
                v.tensor_tensor(q5[:, :, :, 5, :], rest[:, :, 0:H], part2[:, :, 0:H], ALU.subtract)
                v.tensor_tensor(k5[:, :, :, 2, :], rest[:, :, H:], part2[:, :, H:], ALU.subtract)
                for t in range(TB):
                    v.tensor_copy(q5[:, t, :, 0:3, :], part1[:, t, 0:H].unsqueeze(2).to_broadcast([P, H, 3, HD]))
                    v.tensor_copy(q5[:, t, :, 3:5, :], part2[:, t, 0:H].unsqueeze(2).to_broadcast([P, H, 2, HD]))
                for s in (0, 3, 5):
                    v.tensor_copy(k5[:, :, :, s, :], part1[:, :, H:])
                for s in (1, 4):
                    ins = v.tensor_copy(k5[:, :, :, s, :], part2[:, :, H:])
                ins.then_inc(a_stacked, 1)

            def output(n, t):
                o3 = b5[:, 0:OC].rearrange("p (h d) -> p h d", d=HD + 1)
                dve.wait_ge(pv_ready, n + 1)
                link(v.reciprocal(rden[:, :], o3[:, :, HD]))
                wait(dve, o_turned, n)
                v.tensor_tensor(on[:, :].rearrange("p (h d) -> p h d", d=HD), o3[:, :, 0:HD],
                                rden[:, :].unsqueeze(2).to_broadcast([P, H, HD]), ALU.mult).then_inc(o_normed, 1)

            def step(b):
                for t in range(TB):
                    k = b * TB + t
                    c, e, f = k + 1, k - 1, k - 2
                    tc = (t + 1) % TB
                    if has(c, TILES):
                        maxima(c, tc, b)
                    if t == 0 and has(b + 2, B):
                        dve.wait_ge(x1_in, (b + 3) * 16)
                        means((b + 2) * TB, astats, amv, aveps, a_var)
                    if t == 0 and has(b + 1, B):
                        bend(b + 1)
                    if t == 1 and has(b, B):
                        dve.wait_ge(a_vs, b + 1)
                        wait(dve, pv_ready, b * TB)
                        v.tensor_tensor(vsink[:, :], b7[0:H * SINKS, 0:OC], tab["own_head"][0:H * SINKS, :], ALU.mult).then_inc(a_vsink, 1)
                    if t == 1 and has(b + 1, B):
                        stack(b + 1, (b + 1) * TB)
                    if t == 1 and has(b + 2, B):
                        dve.wait_ge(a_rstd, b + 3)
                        wait(dve, a_turned, b + 2)
                        normalise((b + 2) * TB, an, amv, arstd, a_xn)
                    if t == 2 and has(b - 1, B):
                        wait(dve, scattered[0], (b - 1) * (16 * TB) + 16 * TB * 4)
                        r_norm(b - 1 + B, (b - 1) * TB, 0)
                    if t == 3 and has(b - 1, B):
                        r_route(b - 1 + B, 0)
                    if has(e, TILES):
                        output(e, (t - 1) % TB)
                    if has(f, TILES):
                        dve.wait_ge(wo_ready, f + 1)
                        xf = tiles(f, 1).rearrange("p a d -> p (a d)")
                        v.tensor_tensor(xf, b7[:, 0:D], xf, ALU.add).then_inc(x_added, 1)
                    if t == 1 and has(b - 1, B):
                        dve.wait_ge(x_added, b * TB)
                        means((b - 1) * TB, stats, mv, veps, r_var)
                    if t == 3 and has(b - 1, B):
                        r_place(b - 1 + B, 0)

            sweep(dve, step, -2, A_LO, A_HI, B + 1, [(chain, ATTENTION_LINKS)])
            experts(1)

        @block.gpsimd
        def _(pool):
            gp = nc.gpsimd
            chain = Count(pool_chain)

            def link(ins):
                ins.then_inc(pool_chain, 1)
                pool.wait_ge(pool_chain, chain.up())

            gp.memset(vaug[:, :, :, HD:HD + 1], 1.0)
            pool.wait_ge(tables_in, 48)

            def rstds(g, ve, r, var, done):
                pool.wait_ge(var, g + 1)
                gp.tensor_tensor(r[:, :], ve[:, :], tab["nhalf"], ALU.pow).then_inc(done, 1)

            def scatter(g, s, phase):
                wait_apart(pool, r_slots, g + 1)
                wait_apart(pool, r_payx, g + 1)
                for t in range(TB):
                    gp.indirect_dma_start(out=slots_d[phase], out_offset=bass.IndirectOffsetOnAxis(ap=slot_i[s][:, t:t + 1], axis=0),
                                          in_=pay[s][:, t, :], in_offset=None, bounds_check=E * CAP - 1, oob_is_err=False).then_inc(scattered[s], 16)

            def route_step(k, j, u):
                if has(k + 2, B):
                    rstds(k + 2, veps, rstd, r_var, r_rstd)
                if has(k, B):
                    if isinstance(k, int) and k == 0:
                        pool.wait_ge(fresh_out[0], 16 * PAIRS)
                    scatter(k, u, 0)

            sweep2(pool, route_step, -2, R_LO, R_HI, B)

            def experts(phase):
                g0 = PAIRS * phase
                to = out_rows if phase else x1_d

                def step(p):
                    wait_apart(pool, e_rows, p + g0 + 1)
                    for c in range(PC):
                        gp.indirect_dma_start(out=to, out_offset=bass.IndirectOffsetOnAxis(ap=ytok[:, c:c + 1], axis=0),
                                              in_=yrow[:, c, :], in_offset=None, bounds_check=TOKENS - 1, oob_is_err=False).then_inc(e_scattered, 16)

                sweep(pool, step, 0, E_LO, E_HI, PAIRS)

            pool.wait_ge(x_copied, 16)
            experts(0)

            def step(b):
                for t in range(TB):
                    k = b * TB + t
                    d = k + 2
                    if t == 1 and has(b + 2, B):
                        rstds(b + 2, aveps, arstd, a_var, a_rstd)
                    if t == 2 and has(b - 1, B):
                        rstds(b - 1 + B, veps, rstd, r_var, r_rstd)
                    if has(d, TILES):
                        pool.wait_ge(a_qkv_copied, (b + (t + 2) // TB) * 2 + 2)
                        wait(pool, pv_ready, k)
                        gp.tensor_copy(vaug[:, (t + 2) % TB, :, 0:HD], vall[:, bass.ds(d, 1)].rearrange("p a k d -> p (a k) d")).then_inc(v_copied, 1)
                    if t == 0 and has(b - 2, B):
                        scatter(b - 2 + B, 0, 1)
                    if t == 3 and has(b + 2, B):
                        pool.wait_ge(a_qkv_copied, b * 2 + 6)
                        wait(pool, a_stacked, b + 2)
                        half = HD // 2
                        gp.tensor_tensor(roped[:], qkv[:], cos4.unsqueeze(2).to_broadcast([P, TB, H + KV, HD]), ALU.mult)
                        gp.tensor_tensor(rtmp[:, :, :, 0:half], qkv[:, :, :, half:], sin4[:, :, 0:half].unsqueeze(2).to_broadcast([P, TB, H + KV, half]), ALU.mult)
                        link(gp.tensor_tensor(rtmp[:, :, :, half:], qkv[:, :, :, 0:half], sin4[:, :, half:].unsqueeze(2).to_broadcast([P, TB, H + KV, half]), ALU.mult))
                        gp.tensor_tensor(roped[:], roped[:], rtmp[:], ALU.add).then_inc(a_roped, 1)

            pool.wait_ge(fresh_out[1], 16 * PAIRS)
            sweep(pool, step, -2, A_LO, A_HI, B + 2, [(chain, 1)])
            pool.wait_ge(out_written, 16 * B)
            experts(1)


ROUTE_LINKS = 12
ATTENTION_LINKS = 44


_INS = ["L0_attn_x", "L0_attn_Wq", "L0_attn_Wk", "L0_attn_Wv", "L0_attn_Wo", "L0_attn_head_scales", "L0_attn_head_dirs",
        "L0_ffn_gate_w", "L0_ffn_w1", "L0_ffn_w2"]


def kernel(**inputs):
    import numpy as _np
    import concourse.bacc as _bacc
    from concourse import mybir as _mybir
    from concourse.bass_utils import run_bass_kernel_spmd as _run

    nc = _bacc.Bacc("TRN2", target_bir_lowering=False, num_devices=1)
    arrays, args = {}, []
    for name in _INS:
        a = _np.ascontiguousarray(inputs[name])
        arrays[f"in_{name}"] = a
        args.append(nc.dram_tensor(f"in_{name}", a.shape, _mybir.dt.from_np(a.dtype), kind="ExternalInput").ap())
    out = nc.dram_tensor("out", (B, T, D), F32, kind="ExternalOutput").ap()
    macaron(nc, *args, out)
    r = _run(nc, [arrays], core_ids=[0])
    return r.results[0]["out"]
```

```python
from contextlib import ExitStack

import numpy as np

import concourse.bass as bass
from concourse import mybir

F32 = mybir.dt.float32
BF16 = mybir.dt.bfloat16
I32 = mybir.dt.int32
ALU = mybir.AluOpType
ACT = mybir.ActivationFunctionType
X = mybir.AxisListType.X

P = 128
B, T, D = 8, 512, 128
TOKENS = B * T
TILES = TOKENS // P
TB = T // P
H, KV, HD = 8, 4, 16
G = H // KV
SINKS = 4
E, FF = 16, 512
CAP = 320
PAIRS = E // 2
HALF = P // 2
PC = 2 * CAP // P
FC = FF // P
ROW = D + 4
MEAN, RSTD, WEIGHT, TOKEN = D, D + 1, D + 2, D + 3
NOWHERE = 8000.0
EPS = 1e-5
SCALE = 0.25
MASKED = -1e30
Q_PARTS = (0, 0, 0, 1, 1, 2)
K_PARTS = (1, 0, 2, 0, 1, 0)
NP = len(Q_PARTS)
KR = NP * HD
MR = KV * 3
DG = KV * HD


def constants():
    p = np.arange(P)
    q = np.arange(P)
    f, cols = {}, {}

    def add(name, a):
        a = np.ascontiguousarray(a, np.float32).reshape(P, -1)
        f[name] = a
        cols[name] = a.shape[1]

    add("ident", np.eye(P))
    inv_freq = (np.float32(1.0) / np.float32(10000.0) ** (np.arange(0, HD, 2, dtype=np.float32) / np.float32(HD))).astype(np.float32)
    pos = (np.arange(TB)[None, :] * P + p[:, None]).astype(np.float32)
    ang = (pos[:, :, None] * inv_freq[None, None, :]).astype(np.float32)
    cos, sin = np.cos(ang), np.sin(ang)
    add("cos", np.concatenate([cos, cos], -1))
    add("sin", np.concatenate([-sin, sin], -1))
    add("descend", np.broadcast_to(E - np.arange(E), (P, E)))
    add("base", np.broadcast_to(np.arange(E) * CAP - 1, (P, E)))
    add("token", np.arange(TB)[None, :] * P + p[:, None])
    add("nhalf", np.full((P, TB), -0.5))
    row = np.arange(P)[:, None]
    head = np.arange(KV)[:, None] * G + np.arange(G)[None, :]
    own_head = (row // SINKS)[:, :, None, None, None] == head.T[None, :, None, :, None]
    add("own_head", np.broadcast_to(own_head, (P, G, 2, KV, HD)))
    add("repeat", (np.arange(H * SINKS)[None, :] % SINKS) == row)
    h, hc = {}, {}

    def addh(name, a):
        h[name] = np.ascontiguousarray(a, np.float32).reshape(P, -1)
        hc[name] = h[name].shape[1]

    addh("identb", np.eye(P))
    prev = np.where(p[None, :] > q[:, None], 0.0, MASKED)
    own = np.where(p[None, :] <= q[:, None], 0.0, MASKED)
    addh("window", np.concatenate([prev, own], 1))
    addh("turned_window", np.concatenate([prev.T, own.T], 1))
    addh("sink1", np.where(np.arange(SINKS)[None, :] <= q[:, None], 0.0, MASKED))
    addh("upto", p[:, None] <= p[None, :])
    addh("ones", np.ones((P, P)))
    at, ath, o = {}, {}, 0
    for k, c in cols.items():
        at[k] = (o, o + c)
        o += c
    o = 0
    for k, c in hc.items():
        ath[k] = (o, o + c)
        o += c
    rows = np.zeros((MR, KV, T), np.float32)
    for r in range(MR):
        rows[r, r // 3] = 1.0
    fresh = np.zeros((P, PC, ROW), np.float32)
    fresh[:, :, TOKEN] = NOWHERE
    bf16 = mybir.dt.np(BF16)
    return (np.concatenate(list(f.values()), 1), at, np.concatenate(list(h.values()), 1).astype(bf16), ath,
            rows.astype(bf16), fresh)


class Count:

    def __init__(self, sem):
        self.sem, self.base, self.local, self.turn = sem, 0, 0, None

    def enter(self, turn, per):
        self.base, self.local, self.turn, self.per = self.value(), 0, turn, per

    def leave(self, turns):
        assert self.local == self.per, (self.sem, self.local, self.per)
        self.base, self.local, self.turn = self.base + turns * self.per, 0, None

    def value(self):
        at = self.base + self.local
        return at if self.turn is None else self.turn * self.per + at

    def up(self):
        self.local += 1
        return self.value()


class Bank:

    def __init__(self):
        self.last = None

    def take(self, eng, i, sem, reads, wait=lambda eng, s, value: eng.wait_ge(s, value)):
        if self.last is not None:
            s, value, at = self.last
            v = value(at if isinstance(at, int) == isinstance(i, int) else i - 1)
            if not isinstance(v, int) or v > 0:
                wait(eng, s, v)
        self.last = (sem, reads, i)

    def drain(self, eng, i):
        s, value, at = self.last
        eng.wait_ge(s, value(at if isinstance(at, int) else i - 1))


def macaron(nc, x, Wq, Wk, Wv, Wo, head_scales, head_dirs, gate_w, w1, w2, out):
    cf, at, ch, ath, kr_ones, fresh_rows = constants()
    cf_d = nc.inline_tensor(cf, "tables")
    ch_d = nc.inline_tensor(ch, "tables16")
    ones_d = nc.inline_tensor(kr_ones, "max_rows")
    fresh_d = nc.inline_tensor(fresh_rows, "fresh_rows")
    cf_d, ch_d, ones_d, fresh_d = (a.ap() if hasattr(a, "ap") and callable(a.ap) else a for a in (cf_d, ch_d, ones_d, fresh_d))

    slots_d = [nc.dram_tensor(f"slots{i}", (E * CAP, ROW), F32, kind="Internal").ap() for i in range(2)]
    x1_d = nc.dram_tensor("x1", (TOKENS, D), F32, kind="Internal").ap()
    x_rows = x.rearrange("b t d -> (b t) d")
    out_rows = out.rearrange("b t d -> (b t) d")
    x_b = x.rearrange("b (t p) d -> b p t d", p=P)
    x1_b = x1_d.rearrange("(b t p) d -> b p t d", p=P, t=TB)
    out_b = out.rearrange("b (t p) d -> b p t d", p=P)
    slots_p = [s.rearrange("(a p c) w -> a p c w", p=P, c=PC) for s in slots_d]
    w2_e = w2.rearrange("e (c p) d -> e p c d", p=P)

    ctx = ExitStack()
    with ctx:
        def sb(name, shape, dt=F32):
            return ctx.enter_context(nc.sbuf_tensor(name, shape, dt))

        def sem(name):
            return ctx.enter_context(nc.semaphore(name))

        cft = sb("cft", [P, cf.shape[1]])
        cht = sb("cht", [P, ch.shape[1]], BF16)
        tab = {k: cft[:, a:b] for k, (a, b) in at.items()}
        tab16 = {k: cht[:, a:b] for k, (a, b) in ath.items()}
        ident, identb = tab["ident"], tab16["identb"]
        cos4 = tab["cos"].rearrange("p (t d) -> p t d", t=TB)
        sin4 = tab["sin"].rearrange("p (t d) -> p t d", t=TB)
        fresh = sb("fresh", [P, PC, ROW])
        wqkv = sb("wqkv", [P, 2 * D])
        wo = sb("wo", [P, D])
        gw = sb("gw", [E, D])
        gwT = sb("gwT", [P, E])
        dirs = sb("dirs", [P, H, 3])
        hs4 = sb("hs4", [P, H])
        w1s = [sb(f"w1s{i}", [P, FF]) for i in range(2)]
        w2s = [sb(f"w2s{i}", [P, FC, D]) for i in range(2)]

        xall = sb("xall", [P, TILES, D])

        stats = sb("stats", [P, TB, 6])
        mv = [sb(f"mv{i}", [P, TB, 2]) for i in range(2)]
        veps = sb("veps", [P, TB])
        rstd = [sb(f"rstd{i}", [P, TB]) for i in range(2)]
        xn = sb("xn", [P, TB, D])
        xnT = sb("xnT", [P, TB, P])
        lmax = sb("lmax", [P, TB])
        ldiff = sb("ldiff", [P, TB, E])
        lexp = sb("lexp", [P, TB, E])
        lsum = sb("lsum", [P, TB])
        cand = sb("cand", [P, TB, E])
        first = sb("first", [P, TB])
        onehot = sb("onehot", [P, TB, E], BF16)
        place = sb("place", [P, TB, E])
        base = sb("base", [P, E])
        slot = sb("slot", [P, TB])
        limit = sb("limit", [P, TB])
        valid = sb("valid", [P, TB])
        tok_now = sb("tok_now", [P, TB])
        slot_i = [sb(f"slot_i{i}", [P, TB], I32) for i in range(2)]
        pay = [sb(f"pay{i}", [P, TB, ROW]) for i in range(2)]

        rows = sb("rows", [P, PAIRS, PC, ROW])
        en = sb("en", [P, PC, D])
        enT = sb("enT", [P, PC, P])
        hT = [sb(f"hT{i}", [P, FC, CAP]) for i in range(2)]
        yT = sb("yT", [P, PC, P])
        yrow = sb("yrow", [P, PC, D])
        ytok = sb("ytok", [P, PC], I32)

        astats = sb("astats", [P, TB, 6])
        amv = sb("amv", [P, TB, 2])
        aveps = sb("aveps", [P, TB])
        arstd = sb("arstd", [P, TB])
        an = sb("an", [P, TB, D])
        anT = sb("anT", [P, TB, P])
        qkv = sb("qkv", [P, TB, H + KV, HD])
        vall = sb("vall", [P, TILES, KV, HD])
        vaug = sb("vaug", [P, TB, KV, P + HD])
        vcols = vaug[:].rearrange("p t j c -> p t (j c)")
        roped = sb("roped", [P, TB, H + KV, HD])
        rtmp = sb("rtmp", [P, TB, H + KV, HD])
        dprod = sb("dprod", [P, TB, H, 3])
        dsum = sb("dsum", [P, TB, H])
        dscaled = sb("dscaled", [P, TB, H])
        part1 = sb("part1", [P, TB, H + KV, HD], BF16)
        part2 = sb("part2", [P, TB, H + KV, HD], BF16)
        rest = sb("rest", [P, TB, H + KV, HD])
        qs = sb("qs", [P, TB, H, KR], BF16)
        ks = sb("ks", [P, TB, KV, KR], BF16)
        qT = sb("qT", [KR + MR, KV, G, TB, P], BF16)
        kT = sb("kT", [KR + MR, KV, TB, P], BF16)
        nmx = sb("nmx", [P, H])
        nsink = sb("nsink", [P, H])
        nm = sb("nm", [P, H])
        nrest = sb("nrest", [P, H])
        nm3 = sb("nm3", [P, G, KV, 3], BF16)
        psd = sb("psd", [P, H, SINKS])
        psk = [sb(f"psk{i}", [P, H * SINKS]) for i in range(2)]
        pskT = sb("pskT", [H * SINKS, P])
        vsink = sb("vsink", [H * SINKS, G, P])
        probs = [sb(f"probs{i}", [P, KV, 2, G, P]) for i in range(2)]
        ou = sb("ou", [P, G, P])
        rden = sb("rden", [P, G, KV])
        on = sb("on", [P, D])
        oT = sb("oT", [P, P])

        sc = [ctx.enter_context(nc.psum_tensor(f"sc{i}", [P, 2, 512], F32)) for i in range(2)]
        b4, b5, b6, b7 = (ctx.enter_context(nc.psum_tensor(f"b{i}", [P, 512], F32)) for i in (4, 5, 6, 7))
        hid = [sc[0][:, 0, 0:CAP], sc[0][:, 1, 0:CAP], sc[1][:, 0, 0:CAP], sc[1][:, 1, 0:CAP]]
        yps = [b6[:, 0:CAP], b7[:, 0:CAP]]
        b4h = b4[:, :].bitcast(BF16)
        b6h = b6[:, :].bitcast(BF16)

        tables_in = sem("tables_in")
        weights_in = sem("weights_in")
        fresh_in = sem("fresh_in")
        fresh_out = [sem("fresh_out0"), sem("fresh_out1")]
        x_in = [sem("x_in0"), sem("x_in1")]
        x_copied = sem("x_copied")
        x1_in = sem("x1_in")
        rows_in = sem("rows_in")
        w1_in = [sem("w1a_in"), sem("w1b_in")]
        w2_in = [sem("w2a_in"), sem("w2b_in")]
        out_written = sem("out_written")
        vec_chain = sem("vec_chain")
        pool_chain = sem("pool_chain")
        gw_turned = sem("gw_turned")
        gw_copied = sem("gw_copied")
        weights_scaled = sem("weights_scaled")
        r_var = sem("r_var")
        r_rstd = sem("r_rstd")
        r_xn = sem("r_xn")
        r_turned = sem("r_turned")
        r_xnT = sem("r_xnT")
        r_logits = sem("r_logits")
        r_diff = sem("r_diff")
        r_exp = sem("r_exp")
        r_onehot = sem("r_onehot")
        r_rank = sem("r_rank")
        r_based = sem("r_based")
        r_slots = sem("r_slots")
        r_payx = sem("r_payx")
        scattered = [sem("scattered0"), sem("scattered1")]
        e_xn = sem("e_xn")
        e_turned = sem("e_turned")
        e_xT = sem("e_xT")
        e_hid = sem("e_hid")
        e_gelu = sem("e_gelu")
        e_yps = [sem("e_yps0"), sem("e_yps1")]
        e_yT = [sem("e_yT0"), sem("e_yT1")]
        e_back = sem("e_back")
        e_rows = sem("e_rows")
        e_scattered = sem("e_scattered")
        a_var = sem("a_var")
        a_rstd = sem("a_rstd")
        a_xn = sem("a_xn")
        a_turned = sem("a_turned")
        a_xnT = sem("a_xnT")
        a_qkv = sem("a_qkv")
        a_qkv_copied = sem("a_qkv_copied")
        a_roped = sem("a_roped")
        a_bent = sem("a_bent")
        a_stacked = sem("a_stacked")
        a_vs = sem("a_vs")
        a_vsink = sem("a_vsink")
        q_turned = sem("q_turned")
        q_copied = sem("q_copied")
        k_turned = sem("k_turned")
        k_copied = sem("k_copied")
        v_copied = sem("v_copied")
        s_ready = sem("s_ready")
        s_maxed = sem("s_maxed")
        sink_ready = sem("sink_ready")
        nm_split = sem("nm_split")
        nm_turned = sem("nm_turned")
        nm_copied = sem("nm_copied")
        ps_diff = sem("ps_diff")
        ps_exp = sem("ps_exp")
        ps_turned = sem("ps_turned")
        ps_copied = sem("ps_copied")
        st_ready = sem("st_ready")
        st_exp = sem("st_exp")
        pv_ready = sem("pv_ready")
        u_copied = sem("u_copied")
        u_turned = sem("u_turned")
        o_normed = sem("o_normed")
        o_turned = sem("o_turned")
        o_copied = sem("o_copied")
        wo_ready = sem("wo_ready")
        x_added = sem("x_added")

        N_WEIGHTS = 7
        ST = TB - 1

        def wait(eng, s, value):
            if not isinstance(value, int) or value > 0:
                eng.wait_ge(s, value)

        def wait_apart(eng, s, value):
            if isinstance(value, int):
                return wait(eng, s, value)
            value = eng.to_reg(value)
            eng.wait_ge(tables_in, 48)
            eng.wait_ge(s, value)

        def has(i, n):
            return not isinstance(i, int) or 0 <= i < n

        def sweep(eng, step, start, lo, hi, stop, counts=()):
            for i in range(start, lo):
                step(i)
            with eng.Fori(lo, hi) as i:
                for c, per in counts:
                    c.enter(i - lo, per)
                step(i)
            for c, per in counts:
                c.leave(hi - lo)
            for i in range(hi, stop):
                step(i)

        def sweep2(eng, step, start, lo, hi, stop, counts=()):
            for i in range(start, lo):
                step(i, i // 2, i % 2)
            with eng.Fori(lo // 2, hi // 2) as j:
                for c, per in counts:
                    c.enter(j - lo // 2, per)
                for u in range(2):
                    step(j * 2 + u, j, u)
            for c, per in counts:
                c.leave((hi - lo) // 2)
            for i in range(hi, stop):
                step(i, i // 2, i % 2)

        R_LO, R_HI = 2, B - 2
        E_LO, E_HI = 1, PAIRS - 1
        A_LO, A_HI = 2, B - 3

        def tiles(n, k):
            return xall[:, bass.ds(n, k), :]

        block = ctx.enter_context(nc.Block())

        @block.sync
        def _(sp):
            sp.dma_start(xall[:, 0:TB, :], x_b[0]).then_inc(x_in[0], 16)
            sp.dma_start(cft[:, :], cf_d).then_inc(tables_in, 16)
            sp.dma_start(gw[:, :], gate_w).then_inc(tables_in, 16)
            sp.dma_start(cht[:, :], ch_d).then_inc(tables_in, 16)
            sp.dma_start(fresh[:], fresh_d).then_inc(fresh_in, 16)
            sp.dma_start(xall[:, TB:2 * TB, :], x_b[1]).then_inc(x_in[1], 16)
            sp.wait_ge(fresh_in, 16)
            for a in range(PAIRS):
                sp.dma_start(slots_p[0][a], fresh[:]).then_inc(fresh_out[0], 16)
            for b in range(2, B):
                sp.wait_ge(x_in[b % 2], 16 * (b // 2))
                sp.dma_start(xall[:, TB * b:TB * (b + 1), :], x_b[b]).then_inc(x_in[b % 2], 16)
            for i in range(2):
                sp.dma_start(w1s[i][:, :], w1[i]).then_inc(w1_in[i], 16)
                sp.dma_start(w2s[i][:], w2_e[i]).then_inc(w2_in[i], 16)
            sp.dma_start(wqkv[:, 0:D], Wq).then_inc(weights_in, 16)
            sp.dma_start(wqkv[:, D:D + KV * HD], Wk).then_inc(weights_in, 16)
            sp.dma_start(wqkv[:, D + KV * HD:2 * D], Wv).then_inc(weights_in, 16)
            sp.dma_start(wo[:, :], Wo).then_inc(weights_in, 16)
            sp.dma_start(dirs[:].rearrange("p h c -> p (h c)"),
                         head_dirs.rearrange("h c -> (h c)").unsqueeze(0).to_broadcast([P, H * 3])).then_inc(weights_in, 16)
            sp.dma_start(hs4[:, :], head_scales.unsqueeze(0).to_broadcast([P, H])).then_inc(weights_in, 16)
            sp.dma_start(kT[KR:KR + MR].rearrange("r k t p -> r k (t p)"), ones_d).then_inc(weights_in, 16)
            sp.wait_ge(scattered[1], 2 * 16 * TB)
            sp.dma_start(x1_d, x_rows).then_inc(x_copied, 16)
            for a in range(PAIRS):
                sp.dma_start(slots_p[1][a], fresh[:]).then_inc(fresh_out[1], 16)

            def experts(phase):
                g0 = PAIRS * phase
                sp.wait_ge(scattered[0], 16 * TB * (4 + 8 * phase))
                sp.wait_ge(scattered[1], 16 * TB * 4)
                sp.wait_ge(fresh_out[phase], 16 * PAIRS)
                sp.dma_start(rows[:, 0], slots_p[phase][0]).then_inc(rows_in, 16)

                def step(p):
                    g = p + g0
                    first_pair, last_pair = isinstance(p, int) and p == 0, isinstance(p, int) and p == PAIRS - 1
                    if not last_pair:
                        sp.wait_ge(rows_in, (g + 1) * 16)
                        sp.dma_start(rows[:, bass.ds(p + 1, 1)], slots_p[phase][bass.ds(p + 1, 1)].rearrange("a p c w -> p a c w")).then_inc(rows_in, 16)
                    if not first_pair:
                        sp.wait_ge(e_yps[1], g)
                        sp.dma_start(w2s[1][:], w2_e[bass.ds(p * 2 + 1, 1)].rearrange("e p c d -> (e p) c d")).then_inc(w2_in[1], 16)
                    if last_pair and phase == 1:
                        return
                    nxt = 0 if last_pair else p * 2 + 2
                    sp.wait_ge(e_hid, (g * 2 + 1) * FC)
                    sp.dma_start(w1s[0][:, :], w1[bass.ds(nxt, 1)].rearrange("e p f -> (e p) f")).then_inc(w1_in[0], 16)
                    sp.wait_ge(e_hid, (g * 2 + 2) * FC)
                    sp.dma_start(w1s[1][:, :], w1[bass.ds(nxt + 1, 1)].rearrange("e p f -> (e p) f")).then_inc(w1_in[1], 16)
                    sp.wait_ge(e_yps[0], g + 1)
                    sp.dma_start(w2s[0][:], w2_e[bass.ds(nxt, 1)].rearrange("e p c d -> (e p) c d")).then_inc(w2_in[0], 16)

                sweep(sp, step, 0, E_LO, E_HI, PAIRS)
                if phase == 0:
                    sp.wait_ge(e_yps[1], PAIRS)
                    sp.dma_start(w2s[1][:], w2_e[1]).then_inc(w2_in[1], 16)

            experts(0)
            sp.wait_ge(x_copied, 16)
            sp.wait_ge(e_scattered, 16 * PC * PAIRS)
            for b in range(B):
                wait(sp, x1_in, 16 * b)
                sp.dma_start(xall[:, TB * b:TB * (b + 1), :], x1_b[b]).then_inc(x1_in, 16)
            for b in range(B):
                sp.wait_ge(x_added, TB * (b + 1))
                sp.dma_start(out_b[b], xall[:, TB * b:TB * (b + 1), :]).then_inc(out_written, 16)
            experts(1)
            sp.wait_ge(e_scattered, 2 * 16 * PC * PAIRS)

        @block.tensor
        def _(pe):
            mm, turn = nc.tensor.matmul, nc.tensor.transpose
            bank4, bank6, bank7 = Bank(), Bank(), Bank()

            pe.wait_ge(tables_in, 48)
            bank6.take(pe, 0, gw_copied, lambda i: 1)
            turn(b6[:, 0:E], gw[:, :], ident[0:E, 0:E]).then_inc(gw_turned, 1)

            def r_turn(g, i, g_of):
                pe.wait_ge(r_xn, g + 1)
                bank6.take(pe, i, r_xnT, lambda i: g_of(i) + 1)
                for t in range(TB):
                    last = turn(b6[:, P * t:P * (t + 1)], xn[:, t, :], ident)
                last.then_inc(r_turned, 1)

            def r_logit(g, i, g_of):
                pe.wait_ge(r_xnT, g + 1)
                bank7.take(pe, i, r_diff, lambda i: g_of(i) + 1)
                for t in range(TB):
                    last = mm(b7[:, E * t:E * (t + 1)], xnT[:, t, :], gwT[:, :], start=(t == 0), stop=(t == TB - 1), skip_group_check=True)
                last.then_inc(r_logits, 1)

            def r_ranks(g, i, g_of):
                pe.wait_ge(r_onehot, g + 1)
                bank7.take(pe, i, r_based, lambda i: g_of(i) + 1)
                mm(b7[:, 0:TB * E], tab16["upto"], onehot[:].rearrange("p t e -> p (t e)"), start=True, stop=False, skip_group_check=True)
                for t in range(TB):
                    last = mm(b7[:, E * (t + 1):E * (TB + 1)].rearrange("p (t e) -> p t e", e=E), tab16["ones"],
                              onehot[:, t:t + 1, :].to_broadcast([P, TB - t, E]), start=False, stop=(t == TB - 1), skip_group_check=True)
                last.then_inc(r_rank, 1)

            def route_step(k, j, u):
                if has(k + 1, B):
                    r_turn(k + 1, k, lambda i: i + 1)
                if has(k, B):
                    r_ranks(k, k, lambda i: i)
                if has(k + 1, B):
                    r_logit(k + 1, k, lambda i: i + 1)

            sweep2(pe, route_step, -1, R_LO, R_HI, B)

            def experts(phase):
                g0 = PAIRS * phase

                def turn_in(p):
                    g = p + g0
                    pe.wait_ge(e_xn, g + 1)
                    wait(pe, e_rows, max(g - 2, g0) if isinstance(p, int) else g - 2)
                    for c in range(PC):
                        last = turn(b4[:, P * c:P * (c + 1)] if c < 4 else b5[:, 0:P], en[:, c, :], ident)
                    last.then_inc(e_turned, 1)

                def up(p, a):
                    g = p + g0
                    pe.wait_ge(w1_in[a], (g + 1) * 16)
                    if a == 0:
                        pe.wait_ge(e_xT, g + 1)
                    for f in range(FC):
                        wait(pe, e_gelu, (g * 2 + a - 1) * FC + f + 1)
                        mm(hid[f], w1s[a][:, P * f:P * (f + 1)], enT[:, :, HALF * a:HALF * (a + 1)],
                           start=True, stop=True).then_inc(e_hid, 1)

                def down(p, a):
                    g = p + g0
                    pe.wait_ge(w2_in[a], (g + 1) * 16)
                    wait(pe, e_yT[a], g)
                    for f in range(FC):
                        pe.wait_ge(e_gelu, (g * 2 + a) * FC + f + 1)
                        last = mm(yps[a], w2s[a][:, f, :], hT[a][:, f, :], start=(f == 0), stop=(f == FC - 1))
                    last.then_inc(e_yps[a], 1)

                def turn_back(p):
                    g = p + g0
                    for a in range(2):
                        pe.wait_ge(e_yT[a], g + 1)
                    if has(p + 2, PAIRS):
                        pe.wait_ge(e_xT, g + 3)
                    else:
                        pe.wait_ge(e_rows, g)
                    for c in range(PC):
                        last = turn(b4[:, P * c:P * (c + 1)] if c < 4 else b5[:, 0:P], yT[:, c, :], ident)
                    last.then_inc(e_back, 1)

                def step(p):
                    if has(p, PAIRS):
                        up(p, 0)
                    if has(p - 1, PAIRS):
                        down(p - 1, 1)
                    if has(p, PAIRS):
                        up(p, 1)
                    if has(p + 1, PAIRS):
                        turn_in(p + 1)
                    if has(p, PAIRS):
                        down(p, 0)
                    if has(p - 1, PAIRS):
                        turn_back(p - 1)

                sweep(pe, step, -1, E_LO, E_HI, PAIRS + 1)

            bank6.drain(pe, 0)
            bank7.drain(pe, 0)
            experts(0)
            pe.wait_ge(e_gelu, 2 * PAIRS * FC)
            pe.wait_ge(e_rows, PAIRS)
            for a in range(2):
                pe.wait_ge(e_yT[a], PAIRS)
            pe.wait_ge(weights_in, 16 * N_WEIGHTS)
            pe.wait_ge(weights_scaled, 1)

            def a_turn(bb, b):
                pe.wait_ge(a_xn, bb + 1)
                bank6.take(pe, b, a_xnT, lambda b: b + 4)
                for t in range(TB):
                    last = turn(b6[:, P * t:P * (t + 1)], an[:, t, :], ident)
                last.then_inc(a_turned, 1)

            def a_project(bb, b, half):
                pe.wait_ge(a_xnT, bb + 1)
                bank6.take(pe, b, a_qkv_copied, lambda b: (b + 2) * 2 + half + 1)
                for u in range(2):
                    last = mm(b6[:, 2 * D * u:2 * D * (u + 1)], anT[:, 2 * half + u, :], wqkv[:, :],
                              start=(u == 0), stop=(u == 1), skip_group_check=True)
                last.then_inc(a_qkv, 1)

            def turn_q(n, t, bb, b, d):
                pe.wait_ge(a_stacked, bb * 2 + (t // 2 + 1))
                bank4.take(pe, b, q_copied, lambda b: b * TB + d + 1)
                for h in range(H):
                    last = turn(b4h[0:KR, P * h:P * (h + 1)], qs[:, t, h, :], identb)
                last.then_inc(q_turned, 1)

            def turn_k(n, t, b, d):
                bank4.take(pe, b, k_copied, lambda b: b * TB + d + 1)
                for j in range(KV):
                    last = turn(b4h[0:KR, P * j:P * (j + 1)], ks[:, t, j, :], identb)
                last.then_inc(k_turned, 1)

            def scores(n, t):
                pe.wait_ge(k_copied, n + 1)
                lo = 0 if t else P
                for h in range(2):
                    wait(pe, st_exp, n * 2 + h - 3)
                    for jj in range(2):
                        j = 2 * h + jj
                        bank = sc[h][:, jj, :].rearrange("p (g k) -> p g k", g=G)
                        mm(bank[:, :, lo:2 * P], identb, tab16["window"][:, lo:2 * P].unsqueeze(1).to_broadcast([P, G, 2 * P - lo]),
                           start=True, stop=False, skip_group_check=True)
                        for g in range(G):
                            last = mm(bank[:, g, lo:2 * P], qT[0:KR, j, g, t, :],
                                      kT[0:KR, j, t - 1:t + 1, :] if t else kT[0:KR, j, t, :],
                                      start=False, stop=(g == G - 1), skip_group_check=True)
                    last.then_inc(s_ready, 1)

            def sink_scores(t, b):
                bank7.take(pe, b, ps_diff, lambda b: b * ST + t)
                cols = b7[:, 0:H * SINKS].rearrange("p (h s) -> p h s", s=SINKS)
                if t == 1:
                    mm(cols, identb, tab16["sink1"].unsqueeze(1).to_broadcast([P, H, SINKS]), start=True, stop=False, skip_group_check=True)
                for h in range(H):
                    last = mm(cols[:, h, :], qT[0:KR, h // G, h % G, t, :], kT[0:KR, h // G, 0, 0:SINKS],
                              start=(t > 1 and h == 0), stop=(h == H - 1), skip_group_check=True)
                last.then_inc(sink_ready, 1)

            def turned_scores(n, t, h, more):
                pe.wait_ge(nm_copied, n + 1)
                if more:
                    pe.wait_ge(s_maxed, (n + 1) * 2 + h + 1)
                for jj in range(2):
                    j = 2 * h + jj
                    bank = sc[h][:, jj, :].rearrange("p (b g q) -> p b g q", b=2, g=G)
                    lo = 0 if t else 1
                    mm(bank[:, lo:], identb, tab16["turned_window"].rearrange("p (b q) -> p b q", b=2)[:, lo:].unsqueeze(2).to_broadcast([P, 2 - lo, G, P]),
                       start=True, stop=False, skip_group_check=True)
                    for kb in range(lo, 2):
                        last = mm(bank[:, kb], kT[:, j, t - 1 + kb, :], qT[:, j, :, t, :], start=False, stop=(kb == 1), skip_group_check=True)
                last.then_inc(st_ready, 1)

            def turn_max(n, b, d):
                pe.wait_ge(nm_split, n + 1)
                bank6.take(pe, b, nm_copied, lambda b: b * TB + d + 1)
                for g in range(G):
                    last = turn(b6h[KR:KR + MR, P * g:P * (g + 1)], nm3[:, g].rearrange("p k c -> p (k c)"), identb)
                last.then_inc(nm_turned, 1)

            def turn_sinks(t, bb, b):
                pe.wait_ge(ps_exp, bb * ST + t)
                bank6.take(pe, b, ps_copied, lambda b: b * ST + t if t < ST else b * ST)
                turn(b6[0:H * SINKS, 0:P], psk[t % 2][:, :], ident).then_inc(ps_turned, 1)

            def sink_values(b):
                bank7.take(pe, b, a_vsink, lambda b: b + 1, wait_apart)
                pe.wait_ge(v_copied, b * TB + 1)
                mm(b7[0:H * SINKS, 0:P], tab["repeat"][0:SINKS, :],
                   vaug[0:SINKS, 0, :, 0:P].rearrange("p j (u c) -> p u j c", u=2)[:, :, :, 0:HD], start=True, stop=True).then_inc(a_vs, 1)

            def values(n, t, h, bb):
                if h == 0:
                    pe.wait_ge(v_copied, n + 1)
                    wait(pe, u_copied, n)
                pe.wait_ge(st_exp, n * 2 + h + 1)
                first = 0 if t else 1
                for j in (2 * h, 2 * h + 1):
                    for kb in range(first, 2):
                        last = mm(b5[:, 0:G * P], vcols[:, t - 1 + kb, P * j:P * (j + 1)], probs[t % 2][:, j, kb].rearrange("p g q -> p (g q)"),
                                  start=(j == 0 and kb == first), stop=(t == 0 and j == KV - 1), skip_group_check=True)
                if h == 1:
                    if t:
                        pe.wait_ge(ps_copied, bb * ST + t)
                        pe.wait_ge(a_vsink, bb + 1)
                        for g in range(G):
                            last = mm(b5[:, P * g:P * (g + 1)], vsink[:, g, :], pskT[:, :], start=False, stop=(g == G - 1), skip_group_check=True)
                    last.then_inc(pv_ready, 1)

            def turn_sums(n, b, d):
                pe.wait_ge(u_copied, n + 1)
                bank6.take(pe, b, o_normed, lambda b: b * TB + d + 1)
                for g in range(G):
                    last = turn(b6[:, P * g:P * (g + 1)], ou[:, g, :], ident)
                last.then_inc(u_turned, 1)

            def turn_out(n, b, d):
                pe.wait_ge(o_normed, n + 1)
                bank4.take(pe, b, o_copied, lambda b: b * TB + d + 1)
                turn(b4[:, 0:P], on[:, :], ident).then_inc(o_turned, 1)

            def project(n, b, d):
                pe.wait_ge(o_copied, n + 1)
                bank7.take(pe, b, x_added, lambda b: b * TB + d + 1)
                mm(b7[:, 0:D], oT[:, :], wo[:, :], start=True, stop=True).then_inc(wo_ready, 1)

            def step(b):
                for t in range(TB):
                    k = b * TB + t
                    c, d, e, f = k + 1, k + 2, k - 1, k - 2
                    tc, td, te = (t + 1) % TB, (t + 2) % TB, (t - 1) % TB
                    be, bd = b + (t - 1) // TB, b + (t + 2) // TB
                    if has(c, TILES):
                        scores(c, tc)
                        if tc:
                            sink_scores(tc, b)
                    if has(e, TILES) and te:
                        turn_sinks(te, be, b)
                    if has(d, TILES):
                        turn_q(d, td, bd, b, t + 2)
                    if has(f, TILES):
                        turn_sums(f, b, t - 2)
                    if has(k, TILES):
                        turned_scores(k, t, 0, has(c, TILES))
                    if has(e, TILES):
                        values(e, te, 0, be)
                    if has(d, TILES):
                        turn_k(d, td, b, t + 2)
                    if t == 0 and has(b - 2, B):
                        r_logit(b - 2 + B, b, lambda i: i - 2 + B)
                    if has(k, TILES):
                        turned_scores(k, t, 1, has(c, TILES))
                    if has(f, TILES):
                        turn_out(f, b, t - 2)
                    if has(c, TILES):
                        turn_max(c, b, t + 1)
                    if t == 1 and has(b, B):
                        sink_values(b)
                    if has(e, TILES):
                        values(e, te, 1, be)
                    if t == 1 and has(b - 2, B):
                        r_ranks(b - 2 + B, b, lambda i: i - 2 + B)
                    if t == 3 and has(b - 1, B):
                        r_turn(b - 1 + B, b, lambda i: i - 1 + B)
                    if has(f, TILES):
                        project(f, b, t - 2)
                    if t == 3 and has(b + 3, B):
                        a_turn(b + 3, b)
                    if t < 2 and has(b + 2, B):
                        a_project(b + 2, b, t)

            sweep(pe, step, -3, A_LO, A_HI, B + 2)
            pe.wait_ge(st_exp, 2 * TILES)
            pe.wait_ge(u_copied, TILES)
            bank4.drain(pe, 0)
            bank6.drain(pe, 0)
            bank7.drain(pe, 0)
            experts(1)

        @block.scalar
        def _(act):
            act.wait_ge(gw_turned, 1)
            nc.scalar.copy(gwT[:, :], b6[:, 0:E]).then_inc(gw_copied, 1)

            def r_copy(g):
                act.wait_ge(r_turned, g + 1)
                wait(act, r_logits, g)
                nc.scalar.copy(xnT[:].rearrange("p t c -> p (t c)"), b6[:, :]).then_inc(r_xnT, 1)

            def r_exps(g):
                act.wait_ge(r_diff, g + 1)
                nc.scalar.activation(lexp[:].rearrange("p t e -> p (t e)"), ldiff[:].rearrange("p t e -> p (t e)"), ACT.Exp).then_inc(r_exp, 1)

            def route_step(k, j, u):
                if has(k + 1, B):
                    r_copy(k + 1)
                if has(k, B):
                    r_exps(k)
                    act.wait_ge(x_in[u], j * 16 + 16)
                    wait(act, scattered[u], j * (16 * TB))
                    nc.scalar.copy(pay[u][:, :, 0:D], tiles(k * TB, TB)).then_inc(r_payx, 1)

            sweep2(act, route_step, -1, R_LO, R_HI, B)

            def experts(phase):
                g0 = PAIRS * phase

                def gelus(p, a):
                    g = p + g0
                    wait(act, e_yps[a], g)
                    for f in range(FC):
                        act.wait_ge(e_hid, (g * 2 + a) * FC + f + 1)
                        nc.scalar.activation(hT[a][:, f, :], hid[f], ACT.Gelu_apprx_tanh).then_inc(e_gelu, 1)

                def y_copy(p, a):
                    g = p + g0
                    act.wait_ge(e_yps[a], g + 1)
                    wait(act, e_back, g)
                    nc.scalar.copy(yT[:, :, HALF * a:HALF * (a + 1)], yps[a].rearrange("p (c q) -> p c q", c=PC)).then_inc(e_yT[a], 1)

                def step(p):
                    if has(p, PAIRS):
                        gelus(p, 0)
                    if has(p - 1, PAIRS):
                        y_copy(p - 1, 1)
                    if has(p, PAIRS):
                        gelus(p, 1)
                        y_copy(p, 0)

                sweep(act, step, 0, E_LO, E_HI, PAIRS + 1)

            experts(0)

            def qkv_copy(bb, half):
                act.wait_ge(a_qkv, bb * 2 + half + 1)
                wait(act, a_roped, bb)
                ps = b6[:, :].rearrange("p (u h d) -> p u h d", u=2, d=HD)
                nc.scalar.copy(qkv[:, 2 * half:2 * half + 2], ps[:, :, 0:H + KV])
                nc.scalar.copy(vall[:, bass.ds(bb * TB + 2 * half, 2)].rearrange("p u k d -> p u (k d)"),
                               b6[:, :].rearrange("p (u c) -> p u c", u=2)[:, :, D + KV * HD:]).then_inc(a_qkv_copied, 1)

            def step(b):
                for t in range(TB):
                    k = b * TB + t
                    c, d, e, f = k + 1, k + 2, k - 1, k - 2
                    tc, td, te = (t + 1) % TB, (t + 2) % TB, (t - 1) % TB
                    if has(f, TILES):
                        act.wait_ge(pv_ready, f + 1)
                        wait(act, u_turned, f)
                        nc.scalar.copy(ou[:].rearrange("p g q -> p (g q)"), b5[:, 0:G * P]).then_inc(u_copied, 1)
                    if has(e, TILES) and te:
                        act.wait_ge(ps_turned, (b + (t - 1) // TB) * ST + te)
                        wait(act, pv_ready, e)
                        nc.scalar.copy(pskT[:, :], b6[0:H * SINKS, 0:P]).then_inc(ps_copied, 1)
                    if has(d, TILES):
                        act.wait_ge(q_turned, d + 1)
                        nc.scalar.copy(qT[0:KR, :, :, td, :].rearrange("r k g q -> r (k g) q"),
                                       b4h[0:KR, :].rearrange("r (h q) -> r h q", h=H)).then_inc(q_copied, 1)
                    for h in range(2):
                        if has(k, TILES):
                            act.wait_ge(st_ready, k * 2 + h + 1)
                            wait(act, pv_ready, k - 1)
                            if t:
                                nc.scalar.activation(probs[t % 2][:, 2 * h:2 * h + 2].rearrange("p j b g q -> p j (b g q)"),
                                                     sc[h][:], ACT.Exp).then_inc(st_exp, 1)
                            else:
                                nc.scalar.activation(probs[0][:, 2 * h:2 * h + 2, 1].rearrange("p j g q -> p j (g q)"),
                                                     sc[h][:, :, G * P:2 * G * P], ACT.Exp).then_inc(st_exp, 1)
                        if h == 0 and has(d, TILES):
                            act.wait_ge(k_turned, d + 1)
                            nc.scalar.copy(kT[0:KR, :, td, :], b4h[0:KR, 0:KV * P].rearrange("r (k q) -> r k q", k=KV)).then_inc(k_copied, 1)
                    if has(f, TILES):
                        act.wait_ge(o_turned, f + 1)
                        wait(act, wo_ready, f)
                        nc.scalar.copy(oT[:, :], b4[:, 0:P]).then_inc(o_copied, 1)
                    if has(c, TILES):
                        act.wait_ge(nm_turned, c + 1)
                        nc.scalar.copy(qT[KR:KR + MR, :, :, tc, :].rearrange("r k g q -> r g k q"),
                                       b6h[KR:KR + MR, 0:G * P].rearrange("r (g q) -> r g q", g=G).unsqueeze(2).to_broadcast([MR, G, KV, P])).then_inc(nm_copied, 1)
                        if tc:
                            act.wait_ge(ps_diff, b * ST + tc)
                            wait(act, ps_turned, b * ST + tc - 2)
                            nc.scalar.activation(psk[tc % 2][:, :], psd[:].rearrange("p h s -> p (h s)"), ACT.Exp).then_inc(ps_exp, 1)
                    if t < 2 and has(b + 2, B):
                        qkv_copy(b + 2, t)
                    if t == 3 and has(b - 1, B):
                        r_copy(b - 1 + B)
                    if t == 3 and has(b + 3, B):
                        act.wait_ge(a_turned, b + 4)
                        wait(act, a_qkv, (b + 3) * 2)
                        nc.scalar.copy(anT[:].rearrange("p t c -> p (t c)"), b6[:, :]).then_inc(a_xnT, 1)
                    if t == 0 and has(b - 2, B):
                        wait(act, scattered[0], (b - 2) * (16 * TB) + 16 * TB * 4)
                        nc.scalar.copy(pay[0][:, :, 0:D], tiles((b - 2) * TB, TB)).then_inc(r_payx, 1)
                        r_exps(b - 2 + B)

            sweep(act, step, -3, A_LO, A_HI, B + 2)
            experts(1)

        @block.vector
        def _(dve):
            v = nc.vector
            chain = Count(vec_chain)

            def link(ins, wait=wait):
                ins.then_inc(vec_chain, 1)
                wait(dve, vec_chain, chain.up())

            dve.wait_ge(tables_in, 48)

            def fresh_ranks():
                v.tensor_copy(base[:, :], tab["base"])
                link(v.tensor_copy(tok_now[:, :], tab["token"]))

            def means(n0, st, m, ve, done):
                for t in range(TB):
                    ins = v.bn_stats(st[:, t, :], tiles(n0 + t, 1).rearrange("p a d -> p (a d)"))
                link(ins, wait_apart)
                for t in range(TB):
                    ins = v.bn_aggr(m[:, t, :], st[:, t, :])
                link(ins)
                v.tensor_scalar(ve[:, :], m[:, :, 1], EPS, None, ALU.add).then_inc(done, 1)

            def normalise(n0, dst, m, r, done):
                for t in range(TB):
                    ins = v.tensor_scalar(dst[:, t, :], tiles(n0 + t, 1).rearrange("p a d -> p (a d)"),
                                          m[:, t, 0:1], r[:, t:t + 1], ALU.subtract, ALU.mult)
                ins.then_inc(done, 1)

            def r_norm(g, n0, s):
                dve.wait_ge(r_rstd, g + 1)
                wait(dve, r_turned, g)
                normalise(n0, xn, mv[s], rstd[s], r_xn)

            def r_route(g, s, before):
                logits = b7[:, 0:TB * E].rearrange("p (t e) -> p t e", e=E)
                dve.wait_ge(r_logits, g + 1)
                link(v.tensor_reduce(lmax[:, :], logits, X, ALU.max))
                v.tensor_tensor(ldiff[:], logits, lmax[:, :].unsqueeze(2).to_broadcast([P, TB, E]), ALU.subtract).then_inc(r_diff, 1)
                dve.wait_ge(r_diff, g + 1)
                link(v.scalar_tensor_tensor(cand[:], ldiff[:], 0.0, tab["descend"].unsqueeze(1).to_broadcast([P, TB, E]), ALU.is_equal, ALU.mult))
                link(v.tensor_reduce(first[:, :], cand[:], X, ALU.max))
                v.tensor_tensor(onehot[:], cand[:], first[:, :].unsqueeze(2).to_broadcast([P, TB, E]), ALU.is_equal).then_inc(r_onehot, 1)
                wait(dve, scattered[s], before)
                v.tensor_copy(pay[s][:, :, MEAN], mv[s][:, :, 0])
                v.tensor_copy(pay[s][:, :, RSTD], rstd[s][:, :])
                v.tensor_copy(pay[s][:, :, TOKEN], tok_now[:, :])
                v.tensor_scalar(tok_now[:, :], tok_now[:, :], float(T), None, ALU.add)

            def r_place(g, s):
                dve.wait_ge(r_rank, g + 1)
                link(v.tensor_tensor(place[:], b7[:, 0:TB * E].rearrange("p (t e) -> p t e", e=E),
                                     base[:, :].unsqueeze(1).to_broadcast([P, TB, E]), ALU.add))
                v.tensor_tensor(base[:, :], b7[:, TB * E:(TB + 1) * E], base[:, :], ALU.add).then_inc(r_based, 1)
                link(v.tensor_tensor(place[:], place[:], onehot[:], ALU.mult))
                v.tensor_scalar(limit[:, :], first[:, :], -float(CAP), float((E + 1) * CAP), ALU.mult, ALU.add)
                link(v.tensor_reduce(slot[:, :], place[:], X, ALU.add))
                dve.wait_ge(r_exp, g + 1)
                link(v.tensor_reduce(lsum[:, :], lexp[:], X, ALU.add))
                link(v.tensor_scalar(lsum[:, :], lsum[:, :], 2.0, None, ALU.mult))
                v.reciprocal(pay[s][:, :, WEIGHT], lsum[:, :])
                link(v.tensor_tensor(valid[:, :], slot[:, :], limit[:, :], ALU.is_lt))
                link(v.scalar_tensor_tensor(slot[:, :], slot[:, :], NOWHERE, valid[:, :], ALU.subtract, ALU.mult))
                v.tensor_scalar(slot_i[s][:, :], slot[:, :], NOWHERE, None, ALU.add).then_inc(r_slots, 1)

            def route_step(k, j, u):
                if has(k + 1, B):
                    r_norm(k + 1, (k + 1) * TB, (u + 1) % 2)
                if has(k, B):
                    r_route(k, u, j * (16 * TB))
                if has(k + 2, B):
                    dve.wait_ge(x_in[u], j * 16 + 32)
                    means((k + 2) * TB, stats, mv[u], veps, r_var)
                if has(k, B):
                    r_place(k, u)

            fresh_ranks()
            sweep2(dve, route_step, -2, R_LO, R_HI, B, [(chain, 2 * ROUTE_LINKS)])

            def experts(phase):
                g0 = PAIRS * phase

                def norm(p):
                    g = p + g0
                    dve.wait_ge(rows_in, (g + 1) * 16)
                    wait(dve, e_turned, g)
                    for c in range(PC):
                        r = rows[:, bass.ds(p, 1), c, :].rearrange("p a w -> p (a w)")
                        ins = v.tensor_scalar(en[:, c, :], r[:, 0:D], r[:, MEAN:MEAN + 1], r[:, RSTD:RSTD + 1], ALU.subtract, ALU.mult)
                    ins.then_inc(e_xn, 1)

                def copy_in(p):
                    g = p + g0
                    dve.wait_ge(e_turned, g + 1)
                    wait(dve, e_hid, g * (2 * FC))
                    v.tensor_copy(enT[:, 0:4, :].rearrange("p c q -> p (c q)"), b4[:, :])
                    v.tensor_copy(enT[:, 4, :], b5[:, 0:P]).then_inc(e_xT, 1)

                def add_back(p):
                    g = p + g0
                    wait(dve, e_scattered, g * (16 * PC))
                    r = rows[:, bass.ds(p, 1)].rearrange("p a c w -> p (a c) w")
                    v.tensor_copy(ytok[:, :], r[:, :, TOKEN])
                    dve.wait_ge(e_back, g + 1)
                    for c in range(PC):
                        ins = v.scalar_tensor_tensor(yrow[:, c, :], b4[:, P * c:P * (c + 1)] if c < 4 else b5[:, 0:P],
                                                     r[:, c, WEIGHT:WEIGHT + 1], r[:, c, 0:D], ALU.mult, ALU.add)
                    ins.then_inc(e_rows, 1)

                def step(p):
                    if has(p + 1, PAIRS):
                        norm(p + 1)
                        copy_in(p + 1)
                    if has(p - 1, PAIRS):
                        add_back(p - 1)

                sweep(dve, step, -1, E_LO, E_HI, PAIRS + 1)

            experts(0)
            dve.wait_ge(weights_in, 16 * N_WEIGHTS)
            v.tensor_scalar(wqkv[:, 0:D], wqkv[:, 0:D], SCALE, None, ALU.mult)
            v.tensor_scalar(hs4[:, :], hs4[:, :], 1.0 / SCALE, None, ALU.mult).then_inc(weights_scaled, 1)
            dve.wait_ge(weights_scaled, 1)
            fresh_ranks()

            def maxima(n, t, b):
                for h in range(2):
                    dve.wait_ge(s_ready, n * 2 + h + 1)
                    s4 = sc[h][:].rearrange("p j (g k) -> p j g k", g=G)
                    v.tensor_reduce(nmx[:, 4 * h:4 * h + 4].rearrange("p (j g) -> p j g", g=G), s4 if t else s4[:, :, :, P:2 * P],
                                    X, ALU.max, negate=True).then_inc(s_maxed, 1)
                sinks = b7[:, 0:H * SINKS].rearrange("p (h s) -> p h s", s=SINKS)
                if t:
                    dve.wait_ge(sink_ready, b * ST + t)
                    link(v.tensor_reduce(nsink[:, :], sinks, X, ALU.max, negate=True))
                    link(v.tensor_tensor(nm[:, :], nmx[:, :], nsink[:, :], ALU.min))
                    m = nm
                else:
                    dve.wait_ge(s_maxed, n * 2 + 2)
                    m = nmx
                wait(dve, nm_turned, n)
                m3 = nm3[:].rearrange("p g k c -> p k g c")
                mg = m[:, :].rearrange("p (k g) -> p k g", g=G)
                rg = nrest[:, :].rearrange("p (k g) -> p k g", g=G)
                link(v.tensor_copy(m3[:, :, :, 0], mg))
                link(v.tensor_tensor(rg, mg, m3[:, :, :, 0], ALU.subtract))
                link(v.tensor_copy(m3[:, :, :, 1], rg))
                v.tensor_tensor(m3[:, :, :, 2], rg, m3[:, :, :, 1], ALU.subtract).then_inc(nm_split, 1)
                if t:
                    wait(dve, ps_exp, b * ST + t - 1)
                    v.tensor_tensor(psd[:], sinks, nm[:, :].unsqueeze(2).to_broadcast([P, H, SINKS]), ALU.add).then_inc(ps_diff, 1)

            def bend(bb):
                dve.wait_ge(a_roped, bb + 1)
                q3 = roped[:, :, 0:H, 0:3]
                d4 = dirs[:].unsqueeze(1).to_broadcast([P, TB, H, 3])
                link(v.tensor_tensor(dprod[:], q3, d4, ALU.mult))
                link(v.tensor_reduce(dsum[:], dprod[:], X, ALU.add))
                link(v.tensor_tensor(dscaled[:], dsum[:], hs4[:, :].unsqueeze(1).to_broadcast([P, TB, H]), ALU.mult))
                link(v.tensor_tensor(dprod[:], dscaled[:].unsqueeze(3).to_broadcast([P, TB, H, 3]), d4, ALU.mult))
                link(v.tensor_tensor(q3, q3, dprod[:], ALU.add))
                link(v.tensor_copy(part1[:], roped[:]))
                v.tensor_tensor(rest[:], roped[:], part1[:], ALU.subtract).then_inc(a_bent, 1)

            q5 = qs[:].rearrange("p t h (s d) -> p t h s d", s=NP)
            k5 = ks[:].rearrange("p t h (s d) -> p t h s d", s=NP)

            def stack(bb, half):
                if half == 0:
                    dve.wait_ge(a_bent, bb + 1)
                    link(v.tensor_copy(part2[:], rest[:]))
                wait(dve, k_turned, (bb - 1) * TB + 2 * half + 2)
                two = slice(2 * half, 2 * half + 2)
                v.tensor_tensor(q5[:, two, :, 5, :], rest[:, two, 0:H], part2[:, two, 0:H], ALU.subtract)
                v.tensor_tensor(k5[:, two, :, 2, :], rest[:, two, H:], part2[:, two, H:], ALU.subtract)
                for t in (2 * half, 2 * half + 1):
                    v.tensor_copy(q5[:, t, :, 0:3, :], part1[:, t, 0:H].unsqueeze(2).to_broadcast([P, H, 3, HD]))
                    v.tensor_copy(q5[:, t, :, 3:5, :], part2[:, t, 0:H].unsqueeze(2).to_broadcast([P, H, 2, HD]))
                    v.tensor_copy(k5[:, t, :, 1:6:2, :], part1[:, t, H:].unsqueeze(2).to_broadcast([P, KV, 3, HD]))
                    ins = v.tensor_copy(k5[:, t, :, 0:5:4, :], part2[:, t, H:].unsqueeze(2).to_broadcast([P, KV, 2, HD]))
                ins.then_inc(a_stacked, 1)

            def output(n):
                dve.wait_ge(u_turned, n + 1)
                o5 = b6[:, 0:G * P].rearrange("p (g u j d) -> p g u j d", g=G, u=2, d=HD)
                link(v.reciprocal(rden[:], o5[:, :, 1, :, 0]))
                wait(dve, o_turned, n)
                v.tensor_tensor(on[:, :].rearrange("p (j g d) -> p g j d", g=G, d=HD), o5[:, :, 0],
                                rden[:].unsqueeze(3).to_broadcast([P, G, KV, HD]), ALU.mult).then_inc(o_normed, 1)

            def step(b):
                for t in range(TB):
                    k = b * TB + t
                    c, f = k + 1, k - 2
                    if has(c, TILES):
                        maxima(c, (t + 1) % TB, b)
                    if has(f, TILES):
                        output(f)
                    if t == 0:
                        if has(b + 1, B):
                            stack(b + 1, 0)
                        if has(b - 2, B):
                            r_route(b - 2 + B, 0, (b - 2) * (16 * TB) + 16 * TB * 4)
                    if t == 1:
                        if has(b, B):
                            dve.wait_ge(a_vs, b + 1)
                            wait(dve, pv_ready, b * TB)
                            v.tensor_tensor(vsink[:], b7[0:H * SINKS, 0:P].unsqueeze(1).to_broadcast([H * SINKS, G, P]),
                                            tab["own_head"][0:H * SINKS, :].rearrange("p (g c) -> p g c", g=G), ALU.mult).then_inc(a_vsink, 1)
                        if has(b - 2, B):
                            r_place(b - 2 + B, 0)
                        if has(b + 3, B):
                            dve.wait_ge(x1_in, (b + 4) * 16)
                            means((b + 3) * TB, astats, amv, aveps, a_var)
                    if t == 2:
                        if has(b - 1, B):
                            dve.wait_ge(x_added, b * TB)
                            means((b - 1) * TB, stats, mv[0], veps, r_var)
                        if has(b + 1, B):
                            stack(b + 1, 1)
                        if has(b + 3, B):
                            dve.wait_ge(a_rstd, b + 4)
                            wait(dve, a_turned, b + 3)
                            normalise((b + 3) * TB, an, amv, arstd, a_xn)
                    if t == 3:
                        if has(b - 1, B):
                            r_norm(b - 1 + B, (b - 1) * TB, 0)
                        if has(b + 2, B):
                            bend(b + 2)
                    if has(f, TILES):
                        dve.wait_ge(wo_ready, f + 1)
                        xf = tiles(f, 1).rearrange("p a d -> p (a d)")
                        v.tensor_tensor(xf, b7[:, 0:D], xf, ALU.add).then_inc(x_added, 1)

            sweep(dve, step, -3, A_LO, A_HI, B + 2, [(chain, ATTENTION_LINKS)])
            experts(1)

        @block.gpsimd
        def _(pool):
            gp = nc.gpsimd
            chain = Count(pool_chain)

            def link(ins):
                ins.then_inc(pool_chain, 1)
                pool.wait_ge(pool_chain, chain.up())

            gp.memset(vaug[:], 0.0).then_inc(pool_chain, 1)
            pool.wait_ge(pool_chain, chain.up())
            gp.memset(vaug[:, :, :, DG:DG + HD], 1.0)
            pool.wait_ge(tables_in, 48)

            def rstds(g, ve, r, var, done):
                pool.wait_ge(var, g + 1)
                gp.tensor_tensor(r[:, :], ve[:, :], tab["nhalf"], ALU.pow).then_inc(done, 1)

            def scatter(g, s, phase):
                wait_apart(pool, r_slots, g + 1)
                wait_apart(pool, r_payx, g + 1)
                for t in range(TB):
                    gp.indirect_dma_start(out=slots_d[phase], out_offset=bass.IndirectOffsetOnAxis(ap=slot_i[s][:, t:t + 1], axis=0),
                                          in_=pay[s][:, t, :], in_offset=None, bounds_check=E * CAP - 1, oob_is_err=False).then_inc(scattered[s], 16)

            def route_step(k, j, u):
                if has(k + 2, B):
                    rstds(k + 2, veps, rstd[u], r_var, r_rstd)
                if has(k, B):
                    if isinstance(k, int) and k == 0:
                        pool.wait_ge(fresh_out[0], 16 * PAIRS)
                    scatter(k, u, 0)

            sweep2(pool, route_step, -2, R_LO, R_HI, B)

            def experts(phase):
                g0 = PAIRS * phase
                to = out_rows if phase else x1_d

                def step(p):
                    wait_apart(pool, e_rows, p + g0 + 1)
                    for c in range(PC):
                        gp.indirect_dma_start(out=to, out_offset=bass.IndirectOffsetOnAxis(ap=ytok[:, c:c + 1], axis=0),
                                              in_=yrow[:, c, :], in_offset=None, bounds_check=TOKENS - 1, oob_is_err=False).then_inc(e_scattered, 16)

                sweep(pool, step, 0, E_LO, E_HI, PAIRS)

            pool.wait_ge(x_copied, 16)
            experts(0)

            def rope(bb):
                pool.wait_ge(a_qkv_copied, bb * 2 + 2)
                wait(pool, a_bent, bb)
                half = HD // 2
                gp.tensor_tensor(roped[:], qkv[:], cos4.unsqueeze(2).to_broadcast([P, TB, H + KV, HD]), ALU.mult)
                gp.tensor_tensor(rtmp[:, :, :, 0:half], qkv[:, :, :, half:], sin4[:, :, 0:half].unsqueeze(2).to_broadcast([P, TB, H + KV, half]), ALU.mult)
                link(gp.tensor_tensor(rtmp[:, :, :, half:], qkv[:, :, :, 0:half], sin4[:, :, half:].unsqueeze(2).to_broadcast([P, TB, H + KV, half]), ALU.mult))
                gp.tensor_tensor(roped[:], roped[:], rtmp[:], ALU.add).then_inc(a_roped, 1)

            def step(b):
                for t in range(TB):
                    k = b * TB + t
                    d = k + 2
                    if has(d, TILES):
                        pool.wait_ge(a_qkv_copied, (b + (t + 2) // TB) * 2 + 2)
                        wait(pool, pv_ready, k)
                        gp.tensor_copy(vaug[:, (t + 2) % TB, :, 0:HD], vall[:, bass.ds(d, 1)].rearrange("p a k d -> p (a k) d")).then_inc(v_copied, 1)
                    if t == 1 and has(b + 3, B):
                        rstds(b + 3, aveps, arstd, a_var, a_rstd)
                    if t == 1 and has(b + 2, B):
                        rope(b + 2)
                    if t == 2 and has(b - 1, B):
                        rstds(b - 1 + B, veps, rstd[0], r_var, r_rstd)
                    if t == 3 and has(b - 2, B):
                        scatter(b - 2 + B, 0, 1)

            pool.wait_ge(fresh_out[1], 16 * PAIRS)
            sweep(pool, step, -3, A_LO, A_HI, B + 2, [(chain, 1)])
            pool.wait_ge(out_written, 16 * B)
            experts(1)


ROUTE_LINKS = 12
ATTENTION_LINKS = 43


_INS = ["L0_attn_x", "L0_attn_Wq", "L0_attn_Wk", "L0_attn_Wv", "L0_attn_Wo", "L0_attn_head_scales", "L0_attn_head_dirs",
        "L0_ffn_gate_w", "L0_ffn_w1", "L0_ffn_w2"]


def kernel(**inputs):
    import numpy as _np
    import concourse.bacc as _bacc
    from concourse import mybir as _mybir
    from concourse.bass_utils import run_bass_kernel_spmd as _run

    nc = _bacc.Bacc("TRN2", target_bir_lowering=False, num_devices=1)
    arrays, args = {}, []
    for name in _INS:
        a = _np.ascontiguousarray(inputs[name])
        arrays[f"in_{name}"] = a
        args.append(nc.dram_tensor(f"in_{name}", a.shape, _mybir.dt.from_np(a.dtype), kind="ExternalInput").ap())
    out = nc.dram_tensor("out", (B, T, D), F32, kind="ExternalOutput").ap()
    macaron(nc, *args, out)
    r = _run(nc, [arrays], core_ids=[0])
    return r.results[0]["out"]
```

```python
from contextlib import ExitStack

import numpy as np

import concourse.bass as bass
from concourse import mybir

F32 = mybir.dt.float32
BF16 = mybir.dt.bfloat16
I32 = mybir.dt.int32
ALU = mybir.AluOpType
ACT = mybir.ActivationFunctionType
X = mybir.AxisListType.X

P = 128
B, T, D = 8, 512, 128
TOKENS = B * T
TILES = TOKENS // P
TB = T // P
H, KV, HD = 8, 4, 16
G = H // KV
SINKS = 4
E, FF = 16, 512
CAP = 320
PAIRS = E // 2
HALF = P // 2
PC = 2 * CAP // P
FC = FF // P
ROW = D + 4
MEAN, RSTD, WEIGHT, TOKEN = D, D + 1, D + 2, D + 3
NOWHERE = 8000.0
EPS = 1e-5
SCALE = 0.25
MASKED = -1e30
Q_PARTS = (0, 0, 0, 1, 1, 2)
K_PARTS = (1, 0, 2, 0, 1, 0)
NP = len(Q_PARTS)
KR = NP * HD
MR = KV * 3
DG = KV * HD


def constants():
    p = np.arange(P)
    q = np.arange(P)
    tabs, cols = {}, {}

    def add(name, a):
        a = np.ascontiguousarray(a, np.float32).reshape(P, -1)
        tabs[name] = a
        cols[name] = a.shape[1]

    add("ident", np.eye(P))
    inv_freq = (np.float32(1.0) / np.float32(10000.0) ** (np.arange(0, HD, 2, dtype=np.float32) / np.float32(HD))).astype(np.float32)
    pos = (np.arange(TB)[None, :] * P + p[:, None]).astype(np.float32)
    ang = (pos[:, :, None] * inv_freq[None, None, :]).astype(np.float32)
    cos, sin = np.cos(ang), np.sin(ang)
    add("cos", np.concatenate([cos, cos], -1))
    add("sin", np.concatenate([-sin, sin], -1))
    add("descend", np.broadcast_to(E - np.arange(E), (P, E)))
    add("base", np.broadcast_to(np.arange(E) * CAP - 1, (P, E)))
    add("token", np.arange(TB)[None, :] * P + p[:, None])
    add("nhalf", np.full((P, TB), -0.5))
    row = np.arange(P)[:, None]
    head = np.arange(KV)[:, None] * G + np.arange(G)[None, :]
    own_head = (row // SINKS)[:, :, None, None, None] == head.T[None, :, None, :, None]
    add("own_head", np.broadcast_to(own_head, (P, G, 2, KV, HD)))
    add("repeat", (np.arange(H * SINKS)[None, :] % SINKS) == row)
    tabs16, cols16 = {}, {}
    def addh(name, a):
        tabs16[name] = np.ascontiguousarray(a, np.float32).reshape(P, -1)
        cols16[name] = tabs16[name].shape[1]

    addh("identb", np.eye(P))
    prev = np.where(p[None, :] > q[:, None], 0.0, MASKED)
    own = np.where(p[None, :] <= q[:, None], 0.0, MASKED)
    addh("window", np.concatenate([prev, own], 1))
    addh("turned_window", np.concatenate([prev.T, own.T], 1))
    addh("sink1", np.where(np.arange(SINKS)[None, :] <= q[:, None], 0.0, MASKED))
    addh("upto", p[:, None] <= p[None, :])
    addh("ones", np.ones((P, P)))
    at, ath, o = {}, {}, 0
    for k, c in cols.items():
        at[k] = (o, o + c)
        o += c
    o = 0
    for k, c in cols16.items():
        ath[k] = (o, o + c)
        o += c
    rows = np.zeros((MR, KV, T), np.float32)
    for r in range(MR):
        rows[r, r // 3] = 1.0
    fresh = np.zeros((P, PC, ROW), np.float32)
    fresh[:, :, TOKEN] = NOWHERE
    bf16 = mybir.dt.np(BF16)
    return (np.concatenate(list(tabs.values()), 1), at, np.concatenate(list(tabs16.values()), 1).astype(bf16), ath,
            rows.astype(bf16), fresh)


class Count:

    def __init__(self, sem):
        self.sem, self.base, self.local, self.turn = sem, 0, 0, None

    def enter(self, turn, per):
        self.base, self.local, self.turn, self.per = self.value(), 0, turn, per

    def leave(self, turns):
        assert self.local == self.per, (self.sem, self.local, self.per)
        self.base, self.local, self.turn = self.base + turns * self.per, 0, None

    def value(self):
        at = self.base + self.local
        return at if self.turn is None else self.turn * self.per + at

    def up(self):
        self.local += 1
        return self.value()


class Bank:

    def __init__(self):
        self.last = None

    def take(self, eng, i, sem, reads, wait=lambda eng, s, value: eng.wait_ge(s, value)):
        if self.last is not None:
            s, value, at = self.last
            v = value(at if isinstance(at, int) == isinstance(i, int) else i - 1)
            if not isinstance(v, int) or v > 0:
                wait(eng, s, v)
        self.last = (sem, reads, i)

    def drain(self, eng, i):
        s, value, at = self.last
        eng.wait_ge(s, value(at if isinstance(at, int) else i - 1))


def macaron(nc, x, Wq, Wk, Wv, Wo, head_scales, head_dirs, gate_w, w1, w2, out):
    cf, at, ch, ath, kr_ones, fresh_rows = constants()
    cf_d = nc.inline_tensor(cf, "tables")
    ch_d = nc.inline_tensor(ch, "tables16")
    ones_d = nc.inline_tensor(kr_ones, "max_rows")
    fresh_d = nc.inline_tensor(fresh_rows, "fresh_rows")
    cf_d, ch_d, ones_d, fresh_d = (a.ap() if hasattr(a, "ap") and callable(a.ap) else a for a in (cf_d, ch_d, ones_d, fresh_d))

    slots_d = [nc.dram_tensor(f"slots{i}", (E * CAP, ROW), F32, kind="Internal").ap() for i in range(2)]
    x1_d = nc.dram_tensor("x1", (TOKENS, D), F32, kind="Internal").ap()
    x_rows = x.rearrange("b t d -> (b t) d")
    out_rows = out.rearrange("b t d -> (b t) d")
    x_b = x.rearrange("b (t p) d -> b p t d", p=P)
    x1_b = x1_d.rearrange("(b t p) d -> b p t d", p=P, t=TB)
    out_b = out.rearrange("b (t p) d -> b p t d", p=P)
    slots_p = [s.rearrange("(a p c) w -> a p c w", p=P, c=PC) for s in slots_d]
    w2_e = w2.rearrange("e (c p) d -> e p c d", p=P)

    ctx = ExitStack()
    with ctx:
        def sb(name, shape, dt=F32):
            return ctx.enter_context(nc.sbuf_tensor(name, shape, dt))

        def sem(name):
            return ctx.enter_context(nc.semaphore(name))

        cft = sb("cft", [P, cf.shape[1]])
        cht = sb("cht", [P, ch.shape[1]], BF16)
        tab = {k: cft[:, a:b] for k, (a, b) in at.items()}
        tab16 = {k: cht[:, a:b] for k, (a, b) in ath.items()}
        ident, identb = tab["ident"], tab16["identb"]
        cos4 = tab["cos"].rearrange("p (t d) -> p t d", t=TB)
        sin4 = tab["sin"].rearrange("p (t d) -> p t d", t=TB)
        fresh = sb("fresh", [P, PC, ROW])
        wqkv = sb("wqkv", [P, 2 * D])
        wo = sb("wo", [P, D])
        gw = sb("gw", [E, D])
        gwT = sb("gwT", [P, E])
        dirs = sb("dirs", [P, H, 3])
        hs4 = sb("hs4", [P, H])
        w1s = [sb(f"w1s{i}", [P, FF]) for i in range(2)]
        w2s = [sb(f"w2s{i}", [P, FC, D]) for i in range(2)]

        xall = sb("xall", [P, TILES, D])

        stats = sb("stats", [P, TB, 6])
        mv = [sb(f"mv{i}", [P, TB, 2]) for i in range(2)]
        veps = sb("veps", [P, TB])
        rstd = [sb(f"rstd{i}", [P, TB]) for i in range(2)]
        nbias = sb("nbias", [P, TB])
        xn = sb("xn", [P, TB, D])
        xnT = sb("xnT", [P, TB, P])
        lmax = sb("lmax", [P, TB])
        ldiff = sb("ldiff", [P, TB, E])
        lexp = sb("lexp", [P, TB, E])
        lsum = sb("lsum", [P, TB])
        cand = sb("cand", [P, TB, E])
        first = sb("first", [P, TB])
        onehot = sb("onehot", [P, TB, E], BF16)
        place = sb("place", [P, TB, E])
        base = sb("base", [P, E])
        slot = sb("slot", [P, TB])
        limit = sb("limit", [P, TB])
        valid = sb("valid", [P, TB])
        tok_now = sb("tok_now", [P, TB])
        slot_i = [sb(f"slot_i{i}", [P, TB], I32) for i in range(2)]
        pay = [sb(f"pay{i}", [P, TB, ROW]) for i in range(2)]

        rows = sb("rows", [P, PAIRS, PC, ROW])
        ready = sb("ready", [P, 3])
        en = sb("en", [P, PC, D])
        enT = sb("enT", [P, PC, P])
        hT = [sb(f"hT{i}", [P, FC, CAP]) for i in range(2)]
        yT = sb("yT", [P, PC, P])
        yrow = [sb(f"yrow{i}", [P, PC, D]) for i in range(2)]
        ytok = [sb(f"ytok{i}", [P, PC], I32) for i in range(2)]

        astats = sb("astats", [P, TB, 6])
        amv = sb("amv", [P, TB, 2])
        aveps = sb("aveps", [P, TB])
        arstd = sb("arstd", [P, TB])
        anbias = sb("anbias", [P, TB])
        an = sb("an", [P, TB, D])
        anT = sb("anT", [P, TB, P])
        qkv = sb("qkv", [P, TB, H + KV, HD])
        vall = sb("vall", [P, TILES, KV, HD])
        vaug = sb("vaug", [P, TB, KV, P + HD])
        vcols = vaug[:].rearrange("p t j c -> p t (j c)")
        roped = sb("roped", [P, TB, H + KV, HD])
        rtmp = sb("rtmp", [P, TB, H + KV, HD])
        dprod = sb("dprod", [P, TB, H, 3])
        dsum = sb("dsum", [P, TB, H])
        dscaled = sb("dscaled", [P, TB, H])
        part1 = sb("part1", [P, TB, H + KV, HD], BF16)
        part2 = sb("part2", [P, TB, H + KV, HD], BF16)
        rest = sb("rest", [P, TB, H + KV, HD])
        qs = sb("qs", [P, TB, H, KR], BF16)
        ks = sb("ks", [P, TB, KV, KR], BF16)
        qT = sb("qT", [KR + MR, KV, G, TB, P], BF16)
        kT = sb("kT", [KR + MR, KV, TB, P], BF16)
        mx = sb("mx", [P, H])
        junk = sb("junk", [P, H, 2 * P], BF16)
        nsink = sb("nsink", [P, H])
        nm = sb("nm", [P, H])
        nrest = sb("nrest", [P, H])
        nm3 = sb("nm3", [P, G, KV, 3], BF16)
        psd = sb("psd", [P, H, SINKS])
        psk = [sb(f"psk{i}", [P, H * SINKS]) for i in range(2)]
        pskT = sb("pskT", [H * SINKS, P])
        vsink = sb("vsink", [H * SINKS, G, P])
        probs = [sb(f"probs{i}", [P, KV, 2, G, P]) for i in range(2)]
        ou = sb("ou", [P, G, P])
        rden = sb("rden", [P, G, KV])
        on = sb("on", [P, D])
        oT = sb("oT", [P, P])

        sc = [ctx.enter_context(nc.psum_tensor(f"sc{i}", [P, 2, 512], F32)) for i in range(2)]
        b4, b5, b6, b7 = (ctx.enter_context(nc.psum_tensor(f"b{i}", [P, 512], F32)) for i in (4, 5, 6, 7))
        hid = [sc[0][:, 0, 0:CAP], sc[0][:, 1, 0:CAP], sc[1][:, 0, 0:CAP], sc[1][:, 1, 0:CAP]]
        yps = [b6[:, 0:CAP], b7[:, 0:CAP]]
        b4h = b4[:, :].bitcast(BF16)
        b6h = b6[:, :].bitcast(BF16)

        tables_in = sem("tables_in")
        weights_in = sem("weights_in")
        fresh_in = sem("fresh_in")
        fresh_out = [sem("fresh_out0"), sem("fresh_out1")]
        x_in = [sem("x_in0"), sem("x_in1")]
        x_copied = sem("x_copied")
        x1_in = sem("x1_in")
        rows_in = sem("rows_in")
        w1_in = [sem("w1a_in"), sem("w1b_in")]
        w2_in = [sem("w2a_in"), sem("w2b_in")]
        out_written = sem("out_written")
        vec_chain = sem("vec_chain")
        pool_chain = sem("pool_chain")
        gw_turned = sem("gw_turned")
        gw_copied = sem("gw_copied")
        weights_scaled = sem("weights_scaled")
        r_var = sem("r_var")
        r_rstd = sem("r_rstd")
        r_shift = sem("r_shift")
        r_xn = sem("r_xn")
        r_turned = sem("r_turned")
        r_xnT = sem("r_xnT")
        r_logits = sem("r_logits")
        r_diff = sem("r_diff")
        r_exp = sem("r_exp")
        r_onehot = sem("r_onehot")
        r_rank = sem("r_rank")
        r_based = sem("r_based")
        r_slots = sem("r_slots")
        r_payx = sem("r_payx")
        scattered = [sem("scattered0"), sem("scattered1")]
        e_xn = sem("e_xn")
        e_turned = sem("e_turned")
        e_xT = sem("e_xT")
        e_hid = sem("e_hid")
        e_gelu = sem("e_gelu")
        e_yps = [sem("e_yps0"), sem("e_yps1")]
        e_yT = [sem("e_yT0"), sem("e_yT1")]
        e_back = sem("e_back")
        e_rows = sem("e_rows")
        e_scattered = [sem("e_scattered0"), sem("e_scattered1")]
        a_var = sem("a_var")
        a_rstd = sem("a_rstd")
        a_shift = sem("a_shift")
        a_xn = sem("a_xn")
        a_turned = sem("a_turned")
        a_xnT = sem("a_xnT")
        a_qkv = sem("a_qkv")
        a_qkv_copied = sem("a_qkv_copied")
        a_roped = sem("a_roped")
        a_bent = sem("a_bent")
        a_stacked = sem("a_stacked")
        a_vs = sem("a_vs")
        a_vsink = sem("a_vsink")
        q_turned = sem("q_turned")
        q_copied = sem("q_copied")
        k_turned = sem("k_turned")
        k_copied = sem("k_copied")
        v_copied = sem("v_copied")
        s_ready = sem("s_ready")
        s_maxed = sem("s_maxed")
        sink_ready = sem("sink_ready")
        nm_split = sem("nm_split")
        nm_turned = sem("nm_turned")
        nm_copied = sem("nm_copied")
        ps_diff = sem("ps_diff")
        ps_exp = sem("ps_exp")
        ps_turned = sem("ps_turned")
        ps_copied = sem("ps_copied")
        st_ready = sem("st_ready")
        st_exp = sem("st_exp")
        pv_ready = sem("pv_ready")
        u_copied = sem("u_copied")
        u_turned = sem("u_turned")
        o_normed = sem("o_normed")
        o_turned = sem("o_turned")
        o_copied = sem("o_copied")
        wo_ready = sem("wo_ready")
        x_added = sem("x_added")

        N_WEIGHTS = 7
        ST = TB - 1

        def wait(eng, s, value):
            if not isinstance(value, int) or value > 0:
                eng.wait_ge(s, value)

        def wait_apart(eng, s, value):
            if isinstance(value, int):
                return wait(eng, s, value)
            value = eng.to_reg(value)
            eng.wait_ge(tables_in, 48)
            eng.wait_ge(s, value)

        def has(i, n):
            return not isinstance(i, int) or 0 <= i < n

        def sweep(eng, step, start, lo, hi, stop, counts=()):
            for i in range(start, lo):
                step(i)
            with eng.Fori(lo, hi) as i:
                for c, per in counts:
                    c.enter(i - lo, per)
                step(i)
            for c, per in counts:
                c.leave(hi - lo)
            for i in range(hi, stop):
                step(i)

        def sweep2(eng, step, start, lo, hi, stop, counts=()):
            for i in range(start, lo):
                step(i, i // 2, i % 2)
            with eng.Fori(lo // 2, hi // 2) as j:
                for c, per in counts:
                    c.enter(j - lo // 2, per)
                for u in range(2):
                    step(j * 2 + u, j, u)
            for c, per in counts:
                c.leave((hi - lo) // 2)
            for i in range(hi, stop):
                step(i, i // 2, i % 2)

        R_LO, R_HI = 2, B - 2
        E_LO, E_HI = 1, PAIRS - 1
        E2_LO, E2_HI = 2, PAIRS - 2
        A_LO, A_HI = 2, B - 3

        def last_batch(b):
            return isinstance(b, int) and b == B

        def tiles(n, k):
            return xall[:, bass.ds(n, k), :]

        def rotate(v, link, u):
            half, h = HD // 2, H + KV
            two = slice(2 * u, 2 * u + 2)
            v.tensor_tensor(roped[:, two], qkv[:, two], cos4[:, two].unsqueeze(2).to_broadcast([P, 2, h, HD]), ALU.mult)
            v.tensor_tensor(rtmp[:, two, :, 0:half], qkv[:, two, :, half:], sin4[:, two, 0:half].unsqueeze(2).to_broadcast([P, 2, h, half]), ALU.mult)
            link(v.tensor_tensor(rtmp[:, two, :, half:], qkv[:, two, :, 0:half], sin4[:, two, half:].unsqueeze(2).to_broadcast([P, 2, h, half]), ALU.mult))
            v.tensor_tensor(roped[:, two], roped[:, two], rtmp[:, two], ALU.add).then_inc(a_roped, 1)

        block = ctx.enter_context(nc.Block())

        @block.sync
        def _(sp):
            sp.dma_start(xall[:, 0:TB, :], x_b[0]).then_inc(x_in[0], 16)
            sp.dma_start(cft[:, :], cf_d).then_inc(tables_in, 16)
            sp.dma_start(gw[:, :], gate_w).then_inc(tables_in, 16)
            sp.dma_start(cht[:, :], ch_d).then_inc(tables_in, 16)
            sp.dma_start(fresh[:], fresh_d).then_inc(fresh_in, 16)
            sp.dma_start(xall[:, TB:2 * TB, :], x_b[1]).then_inc(x_in[1], 16)
            for b in range(2, B):
                if b == 4:
                    sp.wait_ge(fresh_in, 16)
                    for a in range(PAIRS):
                        sp.dma_start(slots_p[0][a], fresh[:]).then_inc(fresh_out[0], 16)
                sp.wait_ge(x_in[b % 2], 16 * (b // 2))
                sp.dma_start(xall[:, TB * b:TB * (b + 1), :], x_b[b]).then_inc(x_in[b % 2], 16)
            for i in range(2):
                sp.dma_start(w1s[i][:, :], w1[i]).then_inc(w1_in[i], 16)
                sp.dma_start(w2s[i][:], w2_e[i]).then_inc(w2_in[i], 16)
            sp.dma_start(wqkv[:, 0:D], Wq).then_inc(weights_in, 16)
            sp.dma_start(wqkv[:, D:D + KV * HD], Wk).then_inc(weights_in, 16)
            sp.dma_start(wqkv[:, D + KV * HD:2 * D], Wv).then_inc(weights_in, 16)
            sp.dma_start(wo[:, :], Wo).then_inc(weights_in, 16)
            sp.dma_start(dirs[:].rearrange("p h c -> p (h c)"),
                         head_dirs.rearrange("h c -> (h c)").unsqueeze(0).to_broadcast([P, H * 3])).then_inc(weights_in, 16)
            sp.dma_start(hs4[:, :], head_scales.unsqueeze(0).to_broadcast([P, H])).then_inc(weights_in, 16)
            sp.dma_start(kT[KR:KR + MR].rearrange("r k t p -> r k (t p)"), ones_d).then_inc(weights_in, 16)

            def experts(phase):
                g0 = PAIRS * phase
                sp.wait_ge(scattered[0], 16 * TB * (4 + 8 * phase))
                sp.wait_ge(scattered[1], 16 * TB * 4)
                sp.wait_ge(fresh_out[phase], 16 * PAIRS)
                sp.dma_start(rows[:, 0], slots_p[phase][0]).then_inc(rows_in, 16)
                if phase == 0:
                    sp.dma_start(x1_d, x_rows).then_inc(x_copied, 16)

                def step(p):
                    g = p + g0
                    first_pair, last_pair = isinstance(p, int) and p == 0, isinstance(p, int) and p == PAIRS - 1
                    if not last_pair:
                        sp.wait_ge(rows_in, (g + 1) * 16)
                        sp.dma_start(rows[:, bass.ds(p + 1, 1)], slots_p[phase][bass.ds(p + 1, 1)].rearrange("a p c w -> p a c w")).then_inc(rows_in, 16)
                    if not first_pair:
                        sp.wait_ge(e_yps[1], g)
                        sp.dma_start(w2s[1][:], w2_e[bass.ds(p * 2 + 1, 1)].rearrange("e p c d -> (e p) c d")).then_inc(w2_in[1], 16)
                    if last_pair and phase == 1:
                        return
                    nxt = 0 if last_pair else p * 2 + 2
                    sp.wait_ge(e_hid, (g * 2 + 1) * FC)
                    sp.dma_start(w1s[0][:, :], w1[bass.ds(nxt, 1)].rearrange("e p f -> (e p) f")).then_inc(w1_in[0], 16)
                    sp.wait_ge(e_hid, (g * 2 + 2) * FC)
                    sp.dma_start(w1s[1][:, :], w1[bass.ds(nxt + 1, 1)].rearrange("e p f -> (e p) f")).then_inc(w1_in[1], 16)
                    sp.wait_ge(e_yps[0], g + 1)
                    sp.dma_start(w2s[0][:], w2_e[bass.ds(nxt, 1)].rearrange("e p c d -> (e p) c d")).then_inc(w2_in[0], 16)

                sweep(sp, step, 0, E_LO, E_HI, PAIRS)
                if phase == 0:
                    sp.wait_ge(e_yps[1], PAIRS)
                    sp.dma_start(w2s[1][:], w2_e[1]).then_inc(w2_in[1], 16)

            experts(0)
            sp.wait_ge(x_copied, 16)
            for u in range(2):
                sp.wait_ge(e_scattered[u], 16 * PC * PAIRS // 2)
            for b in range(B):
                wait(sp, x1_in, 16 * b)
                sp.dma_start(xall[:, TB * b:TB * (b + 1), :], x1_b[b]).then_inc(x1_in, 16)
            for a in range(PAIRS):
                sp.dma_start(slots_p[1][a], fresh[:]).then_inc(fresh_out[1], 16)
            for b in range(B):
                sp.wait_ge(x_added, TB * (b + 1))
                sp.dma_start(out_b[b], xall[:, TB * b:TB * (b + 1), :]).then_inc(out_written, 16)
            experts(1)
            for u in range(2):
                sp.wait_ge(e_scattered[u], 16 * PC * PAIRS)

        @block.tensor
        def _(pe):
            mm, turn = nc.tensor.matmul, nc.tensor.transpose
            bank4, bank5, bank6, bank7 = Bank(), Bank(), Bank(), Bank()

            def warm(n):
                for _ in range(n):
                    mm(sc[1][:, 1, :], identb, cht[:, 0:512], start=True, stop=True)

            pe.wait_ge(tables_in, 48)
            bank6.take(pe, 0, gw_copied, lambda i: 1)
            turn(b6[:, 0:E], gw[:, :], ident[0:E, 0:E]).then_inc(gw_turned, 1)

            def r_turn(g, i, g_of):
                bank4.take(pe, i, r_xnT, lambda i: g_of(i) + 1)
                for t in range(TB):
                    pe.wait_ge(r_xn, g * TB + (t + 1))
                    last = turn(b4[:, P * t:P * (t + 1)], xn[:, t, :], ident)
                last.then_inc(r_turned, 1)

            def r_logit(g, i, g_of, bank, ps):
                pe.wait_ge(r_xnT, g + 1)
                bank.take(pe, i, r_diff, lambda i: g_of(i) + 1)
                for t in range(TB):
                    last = mm(ps[:, E * t:E * (t + 1)], xnT[:, t, :], gwT[:, :], start=(t == 0), stop=(t == TB - 1), skip_group_check=True)
                last.then_inc(r_logits, 1)

            def r_ranks(g, i, g_of):
                pe.wait_ge(r_onehot, g + 1)
                bank7.take(pe, i, r_based, lambda i: g_of(i) + 1)
                mm(b7[:, 0:TB * E], tab16["upto"], onehot[:].rearrange("p t e -> p (t e)"), start=True, stop=False, skip_group_check=True)
                for t in range(TB):
                    last = mm(b7[:, E * (t + 1):E * (TB + 1)].rearrange("p (t e) -> p t e", e=E), tab16["ones"],
                              onehot[:, t:t + 1, :].to_broadcast([P, TB - t, E]), start=False, stop=(t == TB - 1), skip_group_check=True)
                last.then_inc(r_rank, 1)

            def route_step(k, j, u):
                if has(k + 1, B):
                    r_turn(k + 1, k, lambda i: i + 1)
                if has(k, B):
                    r_ranks(k, k, lambda i: i)
                if has(k + 1, B):
                    r_logit(k + 1, k, lambda i: i + 1, bank5, b5)

            sweep2(pe, route_step, -1, R_LO, R_HI, B)

            def experts(phase):
                g0 = PAIRS * phase

                def turn_in(p):
                    g = p + g0
                    wait(pe, e_rows, (max(g - 2, g0) if isinstance(p, int) else g - 2) * PC)
                    for c in range(PC):
                        pe.wait_ge(e_xn, g * PC + (c + 1))
                        last = turn(b4[:, P * c:P * (c + 1)] if c < 4 else b5[:, 0:P], en[:, c, :], ident)
                    last.then_inc(e_turned, 1)

                def up(p, a):
                    g = p + g0
                    pe.wait_ge(w1_in[a], (g + 1) * 16)
                    if a == 0:
                        pe.wait_ge(e_xT, g + 1)
                    for f in range(FC):
                        wait(pe, e_gelu, (g * 2 + a - 1) * FC + f + 1)
                        mm(hid[f], w1s[a][:, P * f:P * (f + 1)], enT[:, :, HALF * a:HALF * (a + 1)],
                           start=True, stop=True).then_inc(e_hid, 1)

                def down(p, a):
                    g = p + g0
                    pe.wait_ge(w2_in[a], (g + 1) * 16)
                    wait(pe, e_yT[a], g)
                    for f in range(FC):
                        pe.wait_ge(e_gelu, (g * 2 + a) * FC + f + 1)
                        last = mm(yps[a], w2s[a][:, f, :], hT[a][:, f, :], start=(f == 0), stop=(f == FC - 1))
                    last.then_inc(e_yps[a], 1)

                def turn_back(p):
                    g = p + g0
                    for a in range(2):
                        pe.wait_ge(e_yT[a], g + 1)
                    if has(p + 2, PAIRS):
                        pe.wait_ge(e_xT, g + 3)
                    else:
                        pe.wait_ge(e_rows, g * PC)
                    for c in range(PC):
                        last = turn(b4[:, P * c:P * (c + 1)] if c < 4 else b5[:, 0:P], yT[:, c, :], ident)
                    last.then_inc(e_back, 1)

                def step(p):
                    if has(p, PAIRS):
                        up(p, 0)
                    if has(p - 1, PAIRS):
                        down(p - 1, 1)
                    if has(p, PAIRS):
                        up(p, 1)
                    if has(p + 1, PAIRS):
                        turn_in(p + 1)
                        if isinstance(p, int) and p == -1:
                            warm(3)
                    elif has(p, PAIRS):
                        turn_back(p - 1)
                    if has(p, PAIRS):
                        down(p, 0)
                    if has(p - 1, PAIRS) and not (isinstance(p, int) and p == PAIRS - 1):
                        turn_back(p - 1)

                pe.wait_ge(scattered[1 - phase], 16 * TB * (4 + 8 * phase))
                warm(8)
                sweep(pe, step, -1, E_LO, E_HI, PAIRS + 1)

            bank4.drain(pe, 0)
            bank5.drain(pe, 0)
            bank6.drain(pe, 0)
            bank7.drain(pe, 0)
            experts(0)
            pe.wait_ge(e_gelu, 2 * PAIRS * FC)
            pe.wait_ge(e_rows, PAIRS * PC)
            for a in range(2):
                pe.wait_ge(e_yT[a], PAIRS)
            pe.wait_ge(weights_in, 16 * N_WEIGHTS)
            pe.wait_ge(weights_scaled, 1)
            pe.wait_ge(x1_in, 16)
            warm(8)

            def a_turn(bb, b):
                bank6.take(pe, b, a_xnT, lambda b: b + 4)
                for t in range(TB):
                    pe.wait_ge(a_xn, bb * TB + (t + 1))
                    last = turn(b6[:, P * t:P * (t + 1)], an[:, t, :], ident)
                last.then_inc(a_turned, 1)

            def a_project(bb, b, half):
                pe.wait_ge(a_xnT, bb + 1)
                bank6.take(pe, b, a_qkv_copied, lambda b: (b + 2) * 2 + half + 1)
                for u in range(2):
                    last = mm(b6[:, 2 * D * u:2 * D * (u + 1)], anT[:, 2 * half + u, :], wqkv[:, :],
                              start=(u == 0), stop=(u == 1), skip_group_check=True)
                last.then_inc(a_qkv, 1)

            def turn_q(n, t, bb, b, d):
                pe.wait_ge(a_stacked, bb * 2 + (t // 2 + 1))
                bank4.take(pe, b, q_copied, lambda b: b * TB + d + 1)
                for h in range(H):
                    last = turn(b4h[0:KR, P * h:P * (h + 1)], qs[:, t, h, :], identb)
                last.then_inc(q_turned, 1)

            def turn_k(n, t, b, d):
                bank4.take(pe, b, k_copied, lambda b: b * TB + d + 1)
                for j in range(KV):
                    last = turn(b4h[0:KR, P * j:P * (j + 1)], ks[:, t, j, :], identb)
                last.then_inc(k_turned, 1)

            def scores(n, t):
                pe.wait_ge(k_copied, n + 1)
                lo = 0 if t else P
                for h in range(2):
                    wait(pe, st_exp, n * 2 + h - 3)
                    for jj in range(2):
                        j = 2 * h + jj
                        bank = sc[h][:, jj, :].rearrange("p (g k) -> p g k", g=G)
                        for g in range(G):
                            last = mm(bank[:, g, lo:2 * P], qT[0:KR, j, g, t, :],
                                      kT[0:KR, j, t - 1:t + 1, :] if t else kT[0:KR, j, t, :],
                                      start=(g == 0), stop=(g == G - 1), skip_group_check=True)
                    last.then_inc(s_ready, 1)

            def sink_scores(t, b):
                bank7.take(pe, b, ps_diff, lambda b: b * ST + t)
                cols = b7[:, 0:H * SINKS].rearrange("p (h s) -> p h s", s=SINKS)
                if t == 1:
                    mm(cols, identb, tab16["sink1"].unsqueeze(1).to_broadcast([P, H, SINKS]), start=True, stop=False, skip_group_check=True)
                for h in range(H):
                    last = mm(cols[:, h, :], qT[0:KR, h // G, h % G, t, :], kT[0:KR, h // G, 0, 0:SINKS],
                              start=(t > 1 and h == 0), stop=(h == H - 1), skip_group_check=True)
                last.then_inc(sink_ready, 1)

            def turned_scores(n, t, h, more):
                pe.wait_ge(nm_copied, n + 1)
                if more:
                    pe.wait_ge(s_maxed, (n + 1) * 2 + h + 1)
                for jj in range(2):
                    j = 2 * h + jj
                    bank = sc[h][:, jj, :].rearrange("p (b g q) -> p b g q", b=2, g=G)
                    lo = 0 if t else 1
                    mm(bank[:, lo:], identb, tab16["turned_window"].rearrange("p (b q) -> p b q", b=2)[:, lo:].unsqueeze(2).to_broadcast([P, 2 - lo, G, P]),
                       start=True, stop=False, skip_group_check=True)
                    for kb in range(lo, 2):
                        last = mm(bank[:, kb], kT[:, j, t - 1 + kb, :], qT[:, j, :, t, :], start=False, stop=(kb == 1), skip_group_check=True)
                last.then_inc(st_ready, 1)

            def turn_max(n, b, d):
                pe.wait_ge(nm_split, n + 1)
                bank6.take(pe, b, nm_copied, lambda b: b * TB + d + 1)
                for g in range(G):
                    last = turn(b6h[KR:KR + MR, P * g:P * (g + 1)], nm3[:, g].rearrange("p k c -> p (k c)"), identb)
                last.then_inc(nm_turned, 1)

            def turn_sinks(t, bb, b):
                pe.wait_ge(ps_exp, bb * ST + t)
                bank6.take(pe, b, ps_copied, lambda b: b * ST + t if t < ST else b * ST)
                turn(b6[0:H * SINKS, 0:P], psk[t % 2][:, :], ident).then_inc(ps_turned, 1)

            def sink_values(b):
                bank7.take(pe, b, a_vsink, lambda b: b + 1, wait_apart)
                pe.wait_ge(v_copied, b * TB + 1)
                mm(b7[0:H * SINKS, 0:P], tab["repeat"][0:SINKS, :],
                   vaug[0:SINKS, 0, :, 0:P].rearrange("p j (u c) -> p u j c", u=2)[:, :, :, 0:HD], start=True, stop=True).then_inc(a_vs, 1)

            def values(n, t, h, bb):
                if h == 0:
                    pe.wait_ge(v_copied, n + 1)
                    wait(pe, u_copied, n)
                pe.wait_ge(st_exp, n * 2 + h + 1)
                first = 0 if t else 1
                for j in (2 * h, 2 * h + 1):
                    for kb in range(first, 2):
                        last = mm(b5[:, 0:G * P], vcols[:, t - 1 + kb, P * j:P * (j + 1)], probs[t % 2][:, j, kb].rearrange("p g q -> p (g q)"),
                                  start=(j == 0 and kb == first), stop=(t == 0 and j == KV - 1), skip_group_check=True)
                if h == 1:
                    if t:
                        pe.wait_ge(ps_copied, bb * ST + t)
                        pe.wait_ge(a_vsink, bb + 1)
                        for g in range(G):
                            last = mm(b5[:, P * g:P * (g + 1)], vsink[:, g, :], pskT[:, :], start=False, stop=(g == G - 1), skip_group_check=True)
                    last.then_inc(pv_ready, 1)

            def turn_sums(n, b, d):
                pe.wait_ge(u_copied, n + 1)
                bank6.take(pe, b, o_normed, lambda b: b * TB + d + 1)
                for g in range(G):
                    last = turn(b6[:, P * g:P * (g + 1)], ou[:, g, :], ident)
                last.then_inc(u_turned, 1)

            def turn_out(n, b, d):
                pe.wait_ge(o_normed, n + 1)
                bank4.take(pe, b, o_copied, lambda b: b * TB + d + 1)
                turn(b4[:, 0:P], on[:, :], ident).then_inc(o_turned, 1)

            def project(n, b, d):
                pe.wait_ge(o_copied, n + 1)
                bank7.take(pe, b, x_added, lambda b: b * TB + d + 1)
                mm(b7[:, 0:D], oT[:, :], wo[:, :], start=True, stop=True).then_inc(wo_ready, 1)

            def step(b):
                for t in range(TB):
                    k = b * TB + t
                    c, d, e, f = k + 1, k + 2, k - 1, k - 2
                    tc, td, te = (t + 1) % TB, (t + 2) % TB, (t - 1) % TB
                    be, bd = b + (t - 1) // TB, b + (t + 2) // TB
                    if t == 1 and has(b, B):
                        sink_values(b)
                    if has(c, TILES):
                        scores(c, tc)
                        if tc:
                            sink_scores(tc, b)
                    if has(e, TILES) and te:
                        turn_sinks(te, be, b)
                    if has(d, TILES):
                        turn_q(d, td, bd, b, t + 2)
                    if has(f, TILES):
                        turn_sums(f, b, t - 2)
                    if has(k, TILES):
                        turned_scores(k, t, 0, has(c, TILES))
                    if has(e, TILES):
                        values(e, te, 0, be)
                    if has(d, TILES):
                        turn_k(d, td, b, t + 2)
                    if has(k, TILES):
                        turned_scores(k, t, 1, has(c, TILES))
                    if t == 0 and has(b - 2, B):
                        r_logit(b - 2 + B, b, lambda i: i - 2 + B, bank7, b7)
                    if t == (1 if last_batch(b) else 2) and has(b - 2, B):
                        r_ranks(b - 2 + B, b, lambda i: i - 2 + B)
                    if has(c, TILES):
                        turn_max(c, b, t + 1)
                    if has(f, TILES):
                        turn_out(f, b, t - 2)
                    if has(e, TILES):
                        values(e, te, 1, be)
                    if t == 3 and has(b - 1, B):
                        r_turn(b - 1 + B, b, lambda i: i - 1 + B)
                    if has(f, TILES):
                        project(f, b, t - 2)
                    if t < 2 and has(b + 2, B):
                        a_project(b + 2, b, t)
                        if t == 1 and isinstance(b, int) and b == -2:
                            warm(5)
                    if t == 3 and has(b + 3, B):
                        a_turn(b + 3, b)
                        if isinstance(b, int) and b < -1:
                            warm(2 if b == -3 else 5)

            sweep(pe, step, -3, A_LO, A_HI, B + 2)
            pe.wait_ge(st_exp, 2 * TILES)
            pe.wait_ge(u_copied, TILES)
            bank4.drain(pe, 0)
            bank6.drain(pe, 0)
            bank7.drain(pe, 0)
            experts(1)

        @block.scalar
        def _(act):
            act.wait_ge(gw_turned, 1)
            nc.scalar.copy(gwT[:, :], b6[:, 0:E]).then_inc(gw_copied, 1)

            def normalise(n0, dst, r, nb, done, which=range(TB)):
                for t in which:
                    nc.scalar.activation(dst[:, t, :], tiles(n0 + t, 1).rearrange("p a d -> p (a d)"), ACT.Identity,
                                         scale=r[:, t:t + 1], bias=nb[:, t:t + 1]).then_inc(done, 1)

            def r_norm_wait(g):
                wait_apart(act, r_turned, g)
                wait_apart(act, r_shift, g + 1)

            def r_copy(g):
                act.wait_ge(r_turned, g + 1)
                wait(act, r_logits, g)
                nc.scalar.copy(xnT[:].rearrange("p t c -> p (t c)"), b4[:, :]).then_inc(r_xnT, 1)

            def r_exps(g):
                act.wait_ge(r_diff, g + 1)
                nc.scalar.activation(lexp[:].rearrange("p t e -> p (t e)"), ldiff[:].rearrange("p t e -> p (t e)"), ACT.Exp).then_inc(r_exp, 1)

            def route_step(k, j, u):
                if has(k + 1, B):
                    r_norm_wait(k + 1)
                    normalise((k + 1) * TB, xn, rstd[(u + 1) % 2], nbias, r_xn)
                    r_copy(k + 1)
                if has(k, B):
                    r_exps(k)
                    wait_apart(act, x_in[u], j * 16 + 16)
                    wait_apart(act, scattered[u], j * (16 * TB))
                    nc.scalar.copy(pay[u][:, :, 0:D], tiles(k * TB, TB)).then_inc(r_payx, 1)

            sweep2(act, route_step, -1, R_LO, R_HI, B)

            def experts(phase):
                g0 = PAIRS * phase

                nc.scalar.activation(ready[:, phase:phase + 1], tab["ident"][:, 0:1], ACT.Gelu_apprx_tanh)

                def gelus(p, a):
                    g = p + g0
                    wait(act, e_yps[a], g)
                    for f in range(FC):
                        act.wait_ge(e_hid, (g * 2 + a) * FC + f + 1)
                        nc.scalar.activation(hT[a][:, f, :], hid[f], ACT.Gelu_apprx_tanh).then_inc(e_gelu, 1)

                def y_copy(p, a):
                    g = p + g0
                    act.wait_ge(e_yps[a], g + 1)
                    wait(act, e_back, g)
                    nc.scalar.copy(yT[:, :, HALF * a:HALF * (a + 1)], yps[a].rearrange("p (c q) -> p c q", c=PC)).then_inc(e_yT[a], 1)

                def step(p):
                    if has(p, PAIRS):
                        gelus(p, 0)
                    if has(p - 1, PAIRS):
                        y_copy(p - 1, 1)
                    if has(p, PAIRS):
                        gelus(p, 1)
                        y_copy(p, 0)

                sweep(act, step, 0, E_LO, E_HI, PAIRS + 1)

            experts(0)

            nc.scalar.activation(ready[:, 2:3], tab["ident"][:, 0:1], ACT.Exp)

            def a_norm_wait(bb):
                wait_apart(act, a_turned, bb)
                wait_apart(act, a_shift, bb + 1)

            def qkv_copy(bb, half):
                act.wait_ge(a_qkv, bb * 2 + half + 1)
                wait(act, a_roped, bb * 2)
                ps = b6[:, :].rearrange("p (u h d) -> p u h d", u=2, d=HD)
                nc.scalar.copy(qkv[:, 2 * half:2 * half + 2], ps[:, :, 0:H + KV])
                nc.scalar.copy(vall[:, bass.ds(bb * TB + 2 * half, 2)].rearrange("p u k d -> p u (k d)"),
                               b6[:, :].rearrange("p (u c) -> p u c", u=2)[:, :, D + KV * HD:]).then_inc(a_qkv_copied, 1)

            def step(b):
                for t in range(TB):
                    k = b * TB + t
                    c, d, e, f = k + 1, k + 2, k - 1, k - 2
                    tc, td, te = (t + 1) % TB, (t + 2) % TB, (t - 1) % TB
                    if has(f, TILES):
                        act.wait_ge(pv_ready, f + 1)
                        wait(act, u_turned, f)
                        nc.scalar.copy(ou[:].rearrange("p g q -> p (g q)"), b5[:, 0:G * P]).then_inc(u_copied, 1)
                    if has(e, TILES) and te:
                        act.wait_ge(ps_turned, (b + (t - 1) // TB) * ST + te)
                        wait(act, pv_ready, e)
                        nc.scalar.copy(pskT[:, :], b6[0:H * SINKS, 0:P]).then_inc(ps_copied, 1)
                    if has(d, TILES):
                        act.wait_ge(q_turned, d + 1)
                        nc.scalar.copy(qT[0:KR, :, :, td, :].rearrange("r k g q -> r (k g) q"),
                                       b4h[0:KR, :].rearrange("r (h q) -> r h q", h=H)).then_inc(q_copied, 1)
                    for h in range(2):
                        if has(k, TILES):
                            act.wait_ge(st_ready, k * 2 + h + 1)
                            wait(act, pv_ready, k - 1)
                            if t:
                                nc.scalar.activation(probs[t % 2][:, 2 * h:2 * h + 2].rearrange("p j b g q -> p j (b g q)"),
                                                     sc[h][:], ACT.Exp).then_inc(st_exp, 1)
                            else:
                                nc.scalar.activation(probs[0][:, 2 * h:2 * h + 2, 1].rearrange("p j g q -> p j (g q)"),
                                                     sc[h][:, :, G * P:2 * G * P], ACT.Exp).then_inc(st_exp, 1)
                        if h == 0 and t == 2 and has(b + 3, B) and has(k, TILES):
                            a_norm_wait(b + 3)
                            normalise((b + 3) * TB, an, arstd, anbias, a_xn, (0, 1))
                        if h == 0 and t == 3 and has(b - 1, B):
                            r_norm_wait(b - 1 + B)
                            normalise((b - 1) * TB, xn, rstd[0], nbias, r_xn, (0, 1))
                        if h == 0 and has(d, TILES):
                            act.wait_ge(k_turned, d + 1)
                            nc.scalar.copy(kT[0:KR, :, td, :], b4h[0:KR, 0:KV * P].rearrange("r (k q) -> r k q", k=KV)).then_inc(k_copied, 1)
                    if has(f, TILES):
                        act.wait_ge(o_turned, f + 1)
                        wait(act, wo_ready, f)
                        nc.scalar.copy(oT[:, :], b4[:, 0:P]).then_inc(o_copied, 1)
                    if t == 2 and has(b + 3, B):
                        if has(k, TILES):
                            normalise((b + 3) * TB, an, arstd, anbias, a_xn, (2, 3))
                        else:
                            a_norm_wait(b + 3)
                            normalise((b + 3) * TB, an, arstd, anbias, a_xn)
                    if t == 3 and has(b - 1, B):
                        normalise((b - 1) * TB, xn, rstd[0], nbias, r_xn, (2, 3))
                    if has(c, TILES):
                        act.wait_ge(nm_turned, c + 1)
                        nc.scalar.copy(qT[KR:KR + MR, :, :, tc, :].rearrange("r k g q -> r g k q"),
                                       b6h[KR:KR + MR, 0:G * P].rearrange("r (g q) -> r g q", g=G).unsqueeze(2).to_broadcast([MR, G, KV, P])).then_inc(nm_copied, 1)
                        if tc:
                            act.wait_ge(ps_diff, b * ST + tc)
                            wait(act, ps_turned, b * ST + tc - 2)
                            nc.scalar.activation(psk[tc % 2][:, :], psd[:].rearrange("p h s -> p (h s)"), ACT.Exp).then_inc(ps_exp, 1)
                    if t < 2 and has(b + 2, B):
                        qkv_copy(b + 2, t)
                    if t == 3 and has(b - 1, B):
                        r_copy(b - 1 + B)
                    if t == 3 and has(b + 3, B):
                        act.wait_ge(a_turned, b + 4)
                        wait(act, a_qkv, (b + 3) * 2)
                        nc.scalar.copy(anT[:].rearrange("p t c -> p (t c)"), b6[:, :]).then_inc(a_xnT, 1)
                    if t == 0 and has(b - 2, B):
                        wait_apart(act, scattered[0], (b - 2) * (16 * TB) + 16 * TB * 4)
                        nc.scalar.copy(pay[0][:, :, 0:D], tiles((b - 2) * TB, TB)).then_inc(r_payx, 1)
                        r_exps(b - 2 + B)

            sweep(act, step, -3, A_LO, A_HI, B + 2)
            experts(1)

        @block.vector
        def _(dve):
            v = nc.vector
            chain = Count(vec_chain)

            def link(ins, wait=wait):
                ins.then_inc(vec_chain, 1)
                wait(dve, vec_chain, chain.up())

            def mark(ins):
                ins.then_inc(vec_chain, 1)
                return chain.up()

            def need(value):
                wait(dve, vec_chain, value)

            dve.wait_ge(tables_in, 48)

            def fresh_ranks():
                v.tensor_copy(base[:, :], tab["base"])
                link(v.tensor_copy(tok_now[:, :], tab["token"]))

            def means(n0, st, m, ve, done):
                for t in range(TB):
                    ins = v.bn_stats(st[:, t, :], tiles(n0 + t, 1).rearrange("p a d -> p (a d)"))
                link(ins, wait_apart)
                for t in range(TB):
                    ins = v.bn_aggr(m[:, t, :], st[:, t, :])
                link(ins)
                v.tensor_scalar(ve[:, :], m[:, :, 1], EPS, None, ALU.add).then_inc(done, 1)

            def shift(m, r, nb, done):
                v.scalar_tensor_tensor(nb[:, :], m[:, :, 0], -1.0, r[:, :], ALU.mult, ALU.mult).then_inc(done, 1)

            def r_shift_of(g, s):
                dve.wait_ge(r_rstd, g + 1)
                wait(dve, r_xn, g * TB)
                shift(mv[s], rstd[s], nbias, r_shift)

            def r_route(g, s, before, ps):
                logits = ps[:, 0:TB * E].rearrange("p (t e) -> p t e", e=E)
                dve.wait_ge(r_logits, g + 1)
                largest = mark(v.tensor_reduce(lmax[:, :], logits, X, ALU.max))
                need(largest)
                v.tensor_tensor(ldiff[:], logits, lmax[:, :].unsqueeze(2).to_broadcast([P, TB, E]), ALU.subtract).then_inc(r_diff, 1)
                dve.wait_ge(r_diff, g + 1)
                candidates = mark(v.scalar_tensor_tensor(cand[:], ldiff[:], 0.0, tab["descend"].unsqueeze(1).to_broadcast([P, TB, E]), ALU.is_equal, ALU.mult))
                need(candidates)
                chosen = mark(v.tensor_reduce(first[:, :], cand[:], X, ALU.max))
                need(chosen)
                v.tensor_tensor(onehot[:], cand[:], first[:, :].unsqueeze(2).to_broadcast([P, TB, E]), ALU.is_equal).then_inc(r_onehot, 1)
                wait(dve, scattered[s], before)
                v.tensor_copy(pay[s][:, :, MEAN], mv[s][:, :, 0])
                v.tensor_copy(pay[s][:, :, RSTD], rstd[s][:, :])
                v.tensor_copy(pay[s][:, :, TOKEN], tok_now[:, :])
                v.tensor_scalar(tok_now[:, :], tok_now[:, :], float(T), None, ALU.add)

            def r_place(g, s):
                dve.wait_ge(r_exp, g + 1)
                mark(v.tensor_reduce(lsum[:, :], lexp[:], X, ALU.add))
                dve.wait_ge(r_rank, g + 1)
                placed = mark(v.tensor_tensor(place[:], b7[:, 0:TB * E].rearrange("p (t e) -> p t e", e=E),
                                              base[:, :].unsqueeze(1).to_broadcast([P, TB, E]), ALU.add))
                v.tensor_scalar(limit[:, :], first[:, :], -float(CAP), float((E + 1) * CAP), ALU.mult, ALU.add)
                need(placed)
                own = mark(v.tensor_tensor(place[:], place[:], onehot[:], ALU.mult))
                v.tensor_tensor(base[:, :], b7[:, TB * E:(TB + 1) * E], base[:, :], ALU.add).then_inc(r_based, 1)
                doubled = mark(v.tensor_scalar(lsum[:, :], lsum[:, :], 2.0, None, ALU.mult))
                need(own)
                slotted = mark(v.tensor_reduce(slot[:, :], place[:], X, ALU.add))
                need(doubled)
                v.reciprocal(pay[s][:, :, WEIGHT], lsum[:, :])
                need(slotted)
                link(v.tensor_tensor(valid[:, :], slot[:, :], limit[:, :], ALU.is_lt))
                link(v.scalar_tensor_tensor(slot[:, :], slot[:, :], NOWHERE, valid[:, :], ALU.subtract, ALU.mult))
                v.tensor_scalar(slot_i[s][:, :], slot[:, :], NOWHERE, None, ALU.add).then_inc(r_slots, 1)

            def route_step(k, j, u):
                if has(k + 1, B):
                    r_shift_of(k + 1, (u + 1) % 2)
                if has(k, B):
                    r_route(k, u, j * (16 * TB), b5)
                if has(k + 2, B):
                    dve.wait_ge(x_in[u], j * 16 + 32)
                    means((k + 2) * TB, stats, mv[u], veps, r_var)
                if has(k, B):
                    r_place(k, u)

            fresh_ranks()
            sweep2(dve, route_step, -2, R_LO, R_HI, B, [(chain, 2 * ROUTE_LINKS)])

            def experts(phase):
                g0 = PAIRS * phase

                def norm(p):
                    g = p + g0
                    dve.wait_ge(rows_in, (g + 1) * 16)
                    wait(dve, e_turned, g)
                    for c in range(PC):
                        r = rows[:, bass.ds(p, 1), c, :].rearrange("p a w -> p (a w)")
                        v.tensor_scalar(en[:, c, :], r[:, 0:D], r[:, MEAN:MEAN + 1], r[:, RSTD:RSTD + 1], ALU.subtract, ALU.mult).then_inc(e_xn, 1)

                def copy_in(p):
                    g = p + g0
                    dve.wait_ge(e_turned, g + 1)
                    wait(dve, e_hid, g * (2 * FC))
                    v.tensor_copy(enT[:, 0:4, :].rearrange("p c q -> p (c q)"), b4[:, :])
                    v.tensor_copy(enT[:, 4, :], b5[:, 0:P]).then_inc(e_xT, 1)

                def add_back(p, u, before):
                    g = p + g0
                    wait(dve, e_scattered[u], before * (16 * PC))
                    r = rows[:, bass.ds(p, 1)].rearrange("p a c w -> p (a c) w")
                    v.tensor_copy(ytok[u][:, :], r[:, :, TOKEN])
                    dve.wait_ge(e_back, g + 1)
                    for c in range(PC):
                        v.scalar_tensor_tensor(yrow[u][:, c, :], b4[:, P * c:P * (c + 1)] if c < 4 else b5[:, 0:P],
                                               r[:, c, WEIGHT:WEIGHT + 1], r[:, c, 0:D], ALU.mult, ALU.add).then_inc(e_rows, 1)

                def step(p, j, u):
                    if has(p + 1, PAIRS):
                        norm(p + 1)
                        copy_in(p + 1)
                    if has(p - 1, PAIRS):
                        add_back(p - 1, (u + 1) % 2, j + (u - 1) + g0 // 2)

                sweep2(dve, step, -1, E2_LO, E2_HI, PAIRS + 1)

            experts(0)
            dve.wait_ge(weights_in, 16 * N_WEIGHTS)
            v.tensor_scalar(wqkv[:, 0:D], wqkv[:, 0:D], SCALE, None, ALU.mult)
            v.tensor_scalar(hs4[:, :], hs4[:, :], 1.0 / SCALE, None, ALU.mult).then_inc(weights_scaled, 1)
            dve.wait_ge(weights_scaled, 1)
            fresh_ranks()

            def maxima(n, t, b):
                for h in range(2):
                    wait_apart(dve, s_ready, n * 2 + h + 1)
                    lo = 0 if t else P
                    for i in range(H // 2):
                        ins = v.tensor_tensor_reduce(junk[:, H // 2 * h + i, lo:], sc[h][:, i // G, 2 * P * (i % G) + lo:2 * P * (i % G + 1)], tab16["window"][:, lo:],
                                                     scale=1.0, scalar=MASKED, op0=ALU.add, op1=ALU.max, accum_out=mx[:, H // 2 * h + i:H // 2 * h + i + 1])
                    ins.then_inc(s_maxed, 1)
                sinks = b7[:, 0:H * SINKS].rearrange("p (h s) -> p h s", s=SINKS)
                if t:
                    dve.wait_ge(sink_ready, b * ST + t)
                    link(v.tensor_reduce(nsink[:, :], sinks, X, ALU.max, negate=True))
                    link(v.scalar_tensor_tensor(nm[:, :], mx[:, :], -1.0, nsink[:, :], ALU.mult, ALU.min))
                else:
                    dve.wait_ge(s_maxed, n * 2 + 2)
                    link(v.tensor_scalar(nm[:, :], mx[:, :], -1.0, None, ALU.mult))
                wait(dve, nm_turned, n)
                m3 = nm3[:].rearrange("p g k c -> p k g c")
                mg = nm[:, :].rearrange("p (k g) -> p k g", g=G)
                rg = nrest[:, :].rearrange("p (k g) -> p k g", g=G)
                link(v.tensor_copy(m3[:, :, :, 0], mg))
                link(v.tensor_tensor(rg, mg, m3[:, :, :, 0], ALU.subtract))
                link(v.tensor_copy(m3[:, :, :, 1], rg))
                v.tensor_tensor(m3[:, :, :, 2], rg, m3[:, :, :, 1], ALU.subtract).then_inc(nm_split, 1)
                if t:
                    wait(dve, ps_exp, b * ST + t - 1)
                    v.tensor_tensor(psd[:], sinks, nm[:, :].unsqueeze(2).to_broadcast([P, H, SINKS]), ALU.add).then_inc(ps_diff, 1)

            def bend(bb):
                dve.wait_ge(a_roped, bb * 2 + 2)
                q3 = roped[:, :, 0:H, 0:3]
                d4 = dirs[:].unsqueeze(1).to_broadcast([P, TB, H, 3])
                link(v.tensor_tensor(dprod[:], q3, d4, ALU.mult))
                link(v.tensor_reduce(dsum[:], dprod[:], X, ALU.add))
                link(v.tensor_tensor(dscaled[:], dsum[:], hs4[:, :].unsqueeze(1).to_broadcast([P, TB, H]), ALU.mult))
                link(v.tensor_tensor(dprod[:], dscaled[:].unsqueeze(3).to_broadcast([P, TB, H, 3]), d4, ALU.mult))
                link(v.tensor_tensor(q3, q3, dprod[:], ALU.add))
                link(v.tensor_copy(part1[:], roped[:]))
                v.tensor_tensor(rest[:], roped[:], part1[:], ALU.subtract).then_inc(a_bent, 1)

            q5 = qs[:].rearrange("p t h (s d) -> p t h s d", s=NP)
            k5 = ks[:].rearrange("p t h (s d) -> p t h s d", s=NP)

            def stack(bb, half):
                if half == 0:
                    dve.wait_ge(a_bent, bb + 1)
                    link(v.tensor_copy(part2[:], rest[:]))
                wait(dve, k_turned, (bb - 1) * TB + 2 * half + 2)
                two = slice(2 * half, 2 * half + 2)
                v.tensor_tensor(q5[:, two, :, 5, :], rest[:, two, 0:H], part2[:, two, 0:H], ALU.subtract)
                v.tensor_tensor(k5[:, two, :, 2, :], rest[:, two, H:], part2[:, two, H:], ALU.subtract)
                for t in (2 * half, 2 * half + 1):
                    v.tensor_copy(q5[:, t, :, 0:3, :], part1[:, t, 0:H].unsqueeze(2).to_broadcast([P, H, 3, HD]))
                    v.tensor_copy(q5[:, t, :, 3:5, :], part2[:, t, 0:H].unsqueeze(2).to_broadcast([P, H, 2, HD]))
                    v.tensor_copy(k5[:, t, :, 1:6:2, :], part1[:, t, H:].unsqueeze(2).to_broadcast([P, KV, 3, HD]))
                    ins = v.tensor_copy(k5[:, t, :, 0:5:4, :], part2[:, t, H:].unsqueeze(2).to_broadcast([P, KV, 2, HD]))
                ins.then_inc(a_stacked, 1)

            def add(n):
                dve.wait_ge(wo_ready, n + 1)
                xf = tiles(n, 1).rearrange("p a d -> p (a d)")
                v.tensor_tensor(xf, b7[:, 0:D], xf, ALU.add).then_inc(x_added, 1)

            def output(n):
                dve.wait_ge(u_turned, n + 1)
                o5 = b6[:, 0:G * P].rearrange("p (g u j d) -> p g u j d", g=G, u=2, d=HD)
                link(v.reciprocal(rden[:], o5[:, :, 1, :, 0]))
                wait(dve, o_turned, n)
                v.tensor_tensor(on[:, :].rearrange("p (j g d) -> p g j d", g=G, d=HD), o5[:, :, 0],
                                rden[:].unsqueeze(3).to_broadcast([P, G, KV, HD]), ALU.mult).then_inc(o_normed, 1)

            def step(b):
                for t in range(TB):
                    k = b * TB + t
                    c, f = k + 1, k - 2
                    if t == 1 and has(b, B):
                        dve.wait_ge(a_vs, b + 1)
                        wait(dve, pv_ready, b * TB)
                        v.tensor_tensor(vsink[:], b7[0:H * SINKS, 0:P].unsqueeze(1).to_broadcast([H * SINKS, G, P]),
                                        tab["own_head"][0:H * SINKS, :].rearrange("p (g c) -> p g c", g=G), ALU.mult).then_inc(a_vsink, 1)
                    if t == 2 and has(b + 3, B):
                        dve.wait_ge(a_rstd, b + 4)
                        shift(amv, arstd, anbias, a_shift)
                    if has(c, TILES):
                        maxima(c, (t + 1) % TB, b)
                    if has(f, TILES):
                        output(f)
                    if t == 1 and last_batch(b):
                        r_place(b - 2 + B, 0)
                    if t == 0:
                        if has(b + 1, B):
                            stack(b + 1, 0)
                        if has(b - 2, B):
                            r_route(b - 2 + B, 0, (b - 2) * (16 * TB) + 16 * TB * 4, b7)
                    if t == 1:
                        if has(b + 3, B):
                            dve.wait_ge(x1_in, (b + 4) * 16)
                            wait(dve, a_xn, (b + 3) * TB)
                            means((b + 3) * TB, astats, amv, aveps, a_var)
                        if has(b + 1, B):
                            stack(b + 1, 1)
                    if t == 2:
                        if has(b - 2, B) and not last_batch(b):
                            r_place(b - 2 + B, 0)
                        if has(b - 1, B):
                            dve.wait_ge(x_added, b * TB)
                            dve.wait_ge(r_xn, (b - 1 + B) * TB)
                            means((b - 1) * TB, stats, mv[0], veps, r_var)
                    if t == 3:
                        if has(b - 1, B):
                            r_shift_of(b - 1 + B, 0)
                        if isinstance(b, int) and b == -2:
                            dve.wait_ge(a_qkv_copied, 2)
                            rotate(v, link, 1)
                        if has(b + 2, B):
                            bend(b + 2)
                    if has(f, TILES):
                        add(f)

            sweep(dve, step, -3, A_LO, A_HI, B + 2, [(chain, ATTENTION_LINKS)])
            experts(1)

        @block.gpsimd
        def _(pool):
            gp = nc.gpsimd
            chain = Count(pool_chain)

            def link(ins):
                ins.then_inc(pool_chain, 1)
                pool.wait_ge(pool_chain, chain.up())

            link(gp.memset(vaug[:], 0.0))
            gp.memset(vaug[:, :, :, DG:DG + HD], 1.0)
            pool.wait_ge(tables_in, 48)

            def rstds(g, ve, r, var, done):
                pool.wait_ge(var, g + 1)
                gp.tensor_tensor(r[:, :], ve[:, :], tab["nhalf"], ALU.pow).then_inc(done, 1)

            def scatter(g, s, phase, which=range(TB)):
                wait_apart(pool, r_slots, g + 1)
                wait_apart(pool, r_payx, g + 1)
                for t in which:
                    gp.indirect_dma_start(out=slots_d[phase], out_offset=bass.IndirectOffsetOnAxis(ap=slot_i[s][:, t:t + 1], axis=0),
                                          in_=pay[s][:, t, :], in_offset=None, bounds_check=E * CAP - 1, oob_is_err=False).then_inc(scattered[s], 16)

            def route_step(k, j, u):
                if has(k + 2, B):
                    rstds(k + 2, veps, rstd[u], r_var, r_rstd)
                if has(k, B):
                    if isinstance(k, int) and k == 0:
                        pool.wait_ge(fresh_out[0], 16 * PAIRS)
                    scatter(k, u, 0)

            sweep2(pool, route_step, -2, R_LO, R_HI, B)

            def experts(phase):
                g0 = PAIRS * phase
                to = out_rows if phase else x1_d

                def step(p, j, u):
                    for c in range(PC):
                        wait_apart(pool, e_rows, (p + g0) * PC + (c + 1))
                        gp.indirect_dma_start(out=to, out_offset=bass.IndirectOffsetOnAxis(ap=ytok[u][:, c:c + 1], axis=0),
                                              in_=yrow[u][:, c, :], in_offset=None, bounds_check=TOKENS - 1, oob_is_err=False).then_inc(e_scattered[u], 16)

                sweep2(pool, step, 0, E2_LO, E2_HI, PAIRS)

            pool.wait_ge(x_copied, 16)
            experts(0)

            def rope(bb):
                wait(pool, a_bent, bb)
                for u in range(1 if isinstance(bb, int) and bb == 0 else 2):
                    pool.wait_ge(a_qkv_copied, bb * 2 + u + 1)
                    rotate(gp, link, u)

            def step(b):
                for t in range(TB):
                    k = b * TB + t
                    d = k + 2
                    if has(d, TILES):
                        pool.wait_ge(a_qkv_copied, (b + (t + 2) // TB) * 2 + 2)
                        wait(pool, pv_ready, k)
                        gp.tensor_copy(vaug[:, (t + 2) % TB, :, 0:HD], vall[:, bass.ds(d, 1)].rearrange("p a k d -> p (a k) d")).then_inc(v_copied, 1)
                    if t == 1 and has(b + 3, B):
                        rstds(b + 3, aveps, arstd, a_var, a_rstd)
                    if t == 1 and has(b + 2, B):
                        rope(b + 2)
                    if t == 2 and last_batch(b):
                        scatter(b - 2 + B, 0, 1, (0,))
                    if t == 2 and has(b - 1, B):
                        rstds(b - 1 + B, veps, rstd[0], r_var, r_rstd)
                    if t == 3 and isinstance(b, int) and b == 1:
                        pool.wait_ge(fresh_out[1], 16 * PAIRS)
                    if t == 3 and has(b - 2, B):
                        scatter(b - 2 + B, 0, 1, (1, 2, 3) if last_batch(b) else range(TB))

            sweep(pool, step, -3, A_LO, A_HI, B + 2, [(chain, 2)])
            pool.wait_ge(out_written, 16 * B)
            experts(1)


ROUTE_LINKS = 12
ATTENTION_LINKS = 44


_INS = ["L0_attn_x", "L0_attn_Wq", "L0_attn_Wk", "L0_attn_Wv", "L0_attn_Wo", "L0_attn_head_scales", "L0_attn_head_dirs",
        "L0_ffn_gate_w", "L0_ffn_w1", "L0_ffn_w2"]


def kernel(**inputs):
    import numpy as _np
    import concourse.bacc as _bacc
    from concourse import mybir as _mybir
    from concourse.bass_utils import run_bass_kernel_spmd as _run

    nc = _bacc.Bacc("TRN2", target_bir_lowering=False, num_devices=1)
    arrays, args = {}, []
    for name in _INS:
        a = _np.ascontiguousarray(inputs[name])
        arrays[f"in_{name}"] = a
        args.append(nc.dram_tensor(f"in_{name}", a.shape, _mybir.dt.from_np(a.dtype), kind="ExternalInput").ap())
    out = nc.dram_tensor("out", (B, T, D), F32, kind="ExternalOutput").ap()
    macaron(nc, *args, out)
    r = _run(nc, [arrays], core_ids=[0])
    return r.results[0]["out"]
```
